# Optimizing a Trainium2 kernel written in Bass

```python
import numpy as np
import jax
import jax.numpy as jnp

def _softmax(x, axis=-1):
    return jax.nn.softmax(x, axis=axis)

def _gelu(x):
    return jax.nn.gelu(x, approximate=True)

def _silu(x):
    return jax.nn.silu(x)

def _sigmoid(x):
    return jax.nn.sigmoid(x)

def _layernorm(x, axis=-1, eps=1e-05):
    m = jnp.mean(x, axis=axis, keepdims=True)
    v = jnp.var(x, axis=axis, keepdims=True)
    return (x - m) / jnp.sqrt(v + eps)

def _scatter_add(tgt, idx, src, axis=0):
    return tgt.at[idx].add(src)

def _segment_sum(src, seg, n):
    return jax.ops.segment_sum(src, seg, n)
kernel_name = 'mk_adaln_d1_jaxref_r8_90efab'

def setup_inputs(seed: int=0):
    np.random.seed(seed)
    _w = jnp.asarray

    def _L0_attn_setup():
        import jax, jax.numpy as jnp
        import numpy as np
        BATCH, SEQ, D_MODEL = (2, 256, 128)
        D_STATE, D_CONV = (16, 4)
        DT_RANK = 64

        def _forward(x, conv_w, conv_b, x_proj_dt_w, dt_proj_w, dt_proj_b, B_proj_w, C_proj_w, A_log, D_param):
            B, L, D = x.shape
            xc = jax.lax.conv_general_dilated(x.transpose(0, 2, 1), conv_w, window_strides=(1,), padding=[(D_CONV - 1, 0)], feature_group_count=D, dimension_numbers=('NCH', 'OIH', 'NCH'))
            xc = jax.nn.silu((xc + conv_b[None, :, None]).transpose(0, 2, 1))
            dt = jax.nn.softplus(xc @ x_proj_dt_w.T @ dt_proj_w.T + dt_proj_b)
            B_ssm = xc @ B_proj_w.T
            C_ssm = xc @ C_proj_w.T
            A = -jnp.exp(A_log)
            dA = jnp.exp(dt[..., None] * A)
            dBx = dt[..., None] * B_ssm[:, :, None, :] * xc[..., None]

            def step(h, inp):
                dA_t, dBx_t, C_t = inp
                h = dA_t * h + dBx_t
                y_t = jnp.einsum('bdn,bn->bd', h, C_t)
                return (h, y_t)
            h0 = jnp.zeros((B, D, D_STATE), x.dtype)
            _, ys = jax.lax.scan(step, h0, (dA.transpose(1, 0, 2, 3), dBx.transpose(1, 0, 2, 3), C_ssm.transpose(1, 0, 2)))
            return ys.transpose(1, 0, 2) + D_param * xc
        key = jax.random.key(seed)
        ks = jax.random.split(key, 9)
        x = jax.random.normal(ks[0], (BATCH, SEQ, D_MODEL), jnp.float32)
        conv_w = jax.random.normal(ks[1], (D_MODEL, 1, D_CONV), jnp.float32) * 0.3
        conv_b = jax.random.normal(ks[2], (D_MODEL,), jnp.float32) * 0.1
        x_proj_dt_w = jax.random.normal(ks[3], (DT_RANK, D_MODEL), jnp.float32) * D_MODEL ** (-0.5)
        s = DT_RANK ** (-0.5)
        dt_proj_w = jax.random.uniform(ks[4], (D_MODEL, DT_RANK), jnp.float32, -s, s)
        dt = jnp.exp(jax.random.uniform(ks[5], (D_MODEL,), jnp.float32) * (np.log(0.1) - np.log(0.001)) + np.log(0.001))
        dt_proj_b = dt + jnp.log(-jnp.expm1(-dt))
        B_proj_w = jax.random.normal(ks[6], (D_STATE, D_MODEL), jnp.float32) * D_MODEL ** (-0.5)
        C_proj_w = jax.random.normal(ks[7], (D_STATE, D_MODEL), jnp.float32) * D_MODEL ** (-0.5)
        A_log = jnp.log(jnp.tile(jnp.arange(1, D_STATE + 1, dtype=jnp.float32), (D_MODEL, 1)))
        D_param = jnp.ones((D_MODEL,), jnp.float32)
        return dict(x=x, conv_w=conv_w, conv_b=conv_b, x_proj_dt_w=x_proj_dt_w, dt_proj_w=dt_proj_w, dt_proj_b=dt_proj_b, B_proj_w=B_proj_w, C_proj_w=C_proj_w, A_log=A_log, D_param=D_param)
    _L0_attn_in = _L0_attn_setup()

    def _L0_ffn_setup():
        import jax, jax.numpy as jnp
        import numpy as np
        from jax import lax
        D = 128
        H = 176
        E = 8
        K = 2
        ROUTER_SCALE = 1.0

        def _expert(x, w1, b1, w3, b3, w2, b2):
            h = jax.nn.silu((x @ w1 + b1) * (x @ w3 + b3))
            return h @ w2 + b2
        key = jax.random.key(seed)
        ks = jax.random.split(key, 16)
        s = 0.02
        inp = {'x': jax.random.normal(ks[0], (2, 256, D), dtype=jnp.float32), 'gate_w': jax.random.normal(ks[1], (E, D), dtype=jnp.float32) * s, 'gate_b': jax.random.normal(ks[2], (E,), dtype=jnp.float32) * s, 'w1': jax.random.normal(ks[3], (E, D, H), dtype=jnp.float32) * s, 'b1': jax.random.normal(ks[4], (E, H), dtype=jnp.float32) * s, 'w3': jax.random.normal(ks[5], (E, D, H), dtype=jnp.float32) * s, 'b3': jax.random.normal(ks[6], (E, H), dtype=jnp.float32) * s, 'w2': jax.random.normal(ks[7], (E, H, D), dtype=jnp.float32) * s, 'b2': jax.random.normal(ks[8], (E, D), dtype=jnp.float32) * s, 'sw1': jax.random.normal(ks[9], (D, H), dtype=jnp.float32) * s, 'sb1': jax.random.normal(ks[10], (H,), dtype=jnp.float32) * s, 'sw3': jax.random.normal(ks[11], (D, H), dtype=jnp.float32) * s, 'sb3': jax.random.normal(ks[12], (H,), dtype=jnp.float32) * s, 'sw2': jax.random.normal(ks[13], (H, D), dtype=jnp.float32) * s, 'sb2': jax.random.normal(ks[14], (D,), dtype=jnp.float32) * s}
        return inp
    _L0_ffn_in = _L0_ffn_setup()
    _L0_c = _w((lambda *s: np.random.randn(*s).astype(np.float32) * 0.05)(4, 128))
    _L0_wmod = _w((lambda *s: np.random.randn(*s).astype(np.float32) * 0.05)(128, 6 * 128) * 128 ** (-0.5))
    _d = {'L0_attn_x': _L0_attn_in['x'], 'L0_attn_conv_w': _L0_attn_in['conv_w'], 'L0_attn_conv_b': _L0_attn_in['conv_b'], 'L0_attn_x_proj_dt_w': _L0_attn_in['x_proj_dt_w'], 'L0_attn_dt_proj_w': _L0_attn_in['dt_proj_w'], 'L0_attn_dt_proj_b': _L0_attn_in['dt_proj_b'], 'L0_attn_B_proj_w': _L0_attn_in['B_proj_w'], 'L0_attn_C_proj_w': _L0_attn_in['C_proj_w'], 'L0_attn_A_log': _L0_attn_in['A_log'], 'L0_attn_D_param': _L0_attn_in['D_param'], 'L0_ffn_gate_w': _L0_ffn_in['gate_w'], 'L0_ffn_gate_b': _L0_ffn_in['gate_b'], 'L0_ffn_w1': _L0_ffn_in['w1'], 'L0_ffn_b1': _L0_ffn_in['b1'], 'L0_ffn_w3': _L0_ffn_in['w3'], 'L0_ffn_b3': _L0_ffn_in['b3'], 'L0_ffn_w2': _L0_ffn_in['w2'], 'L0_ffn_b2': _L0_ffn_in['b2'], 'L0_ffn_sw1': _L0_ffn_in['sw1'], 'L0_ffn_sb1': _L0_ffn_in['sb1'], 'L0_ffn_sw3': _L0_ffn_in['sw3'], 'L0_ffn_sb3': _L0_ffn_in['sb3'], 'L0_ffn_sw2': _L0_ffn_in['sw2'], 'L0_ffn_sb2': _L0_ffn_in['sb2'], 'L0_c': _L0_c, 'L0_wmod': _L0_wmod}
    _x0 = _d['L0_attn_x']
    _d['L0_attn_x'] = jax.random.normal(jax.random.fold_in(jax.random.key(seed), 1), (4, 1024, 128), dtype=_x0.dtype)
    del _x0
    return _d

def reference(L0_attn_x, L0_attn_conv_w, L0_attn_conv_b, L0_attn_x_proj_dt_w, L0_attn_dt_proj_w, L0_attn_dt_proj_b, L0_attn_B_proj_w, L0_attn_C_proj_w, L0_attn_A_log, L0_attn_D_param, L0_ffn_gate_w, L0_ffn_gate_b, L0_ffn_w1, L0_ffn_b1, L0_ffn_w3, L0_ffn_b3, L0_ffn_w2, L0_ffn_b2, L0_ffn_sw1, L0_ffn_sb1, L0_ffn_sw3, L0_ffn_sb3, L0_ffn_sw2, L0_ffn_sb2, L0_c, L0_wmod):

    def _L0_attn_ref(x, conv_w, conv_b, x_proj_dt_w, dt_proj_w, dt_proj_b, B_proj_w, C_proj_w, A_log, D_param):
        import jax, jax.numpy as jnp
        import numpy as np
        BATCH, SEQ, D_MODEL = (2, 256, 128)
        D_STATE, D_CONV = (16, 4)
        DT_RANK = 64

        def _forward(x, conv_w, conv_b, x_proj_dt_w, dt_proj_w, dt_proj_b, B_proj_w, C_proj_w, A_log, D_param):
            B, L, D = x.shape
            xc = jax.lax.conv_general_dilated(x.transpose(0, 2, 1), conv_w, window_strides=(1,), padding=[(D_CONV - 1, 0)], feature_group_count=D, dimension_numbers=('NCH', 'OIH', 'NCH'))
            xc = jax.nn.silu((xc + conv_b[None, :, None]).transpose(0, 2, 1))
            dt = jax.nn.softplus(xc @ x_proj_dt_w.T @ dt_proj_w.T + dt_proj_b)
            B_ssm = xc @ B_proj_w.T
            C_ssm = xc @ C_proj_w.T
            A = -jnp.exp(A_log)
            dA = jnp.exp(dt[..., None] * A)
            dBx = dt[..., None] * B_ssm[:, :, None, :] * xc[..., None]

            def step(h, inp):
                dA_t, dBx_t, C_t = inp
                h = dA_t * h + dBx_t
                y_t = jnp.einsum('bdn,bn->bd', h, C_t)
                return (h, y_t)
            h0 = jnp.zeros((B, D, D_STATE), x.dtype)
            _, ys = jax.lax.scan(step, h0, (dA.transpose(1, 0, 2, 3), dBx.transpose(1, 0, 2, 3), C_ssm.transpose(1, 0, 2)))
            return ys.transpose(1, 0, 2) + D_param * xc
        return _forward(x, conv_w, conv_b, x_proj_dt_w, dt_proj_w, dt_proj_b, B_proj_w, C_proj_w, A_log, D_param)

    def _L0_ffn_ref(x, gate_w, gate_b, w1, b1, w3, b3, w2, b2, sw1, sb1, sw3, sb3, sw2, sb2):
        import jax, jax.numpy as jnp
        import numpy as np
        from jax import lax
        D = 128
        H = 176
        E = 8
        K = 2
        ROUTER_SCALE = 1.0

        def _expert(x, w1, b1, w3, b3, w2, b2):
            h = jax.nn.silu((x @ w1 + b1) * (x @ w3 + b3))
            return h @ w2 + b2
        shape = x.shape
        xf = x.reshape(-1, D)
        T = xf.shape[0]
        scores = jax.nn.softmax(xf @ gate_w.T, axis=-1)
        biased = scores + gate_b
        _, idx = lax.top_k(biased, K)
        w = jnp.take_along_axis(scores, idx, axis=-1) * ROUTER_SCALE
        rw = jnp.zeros((T, E), dtype=xf.dtype).at[jnp.arange(T)[:, None], idx].add(w)
        h = jax.nn.silu((jnp.einsum('td,edh->teh', xf, w1) + b1) * (jnp.einsum('td,edh->teh', xf, w3) + b3))
        oe = jnp.einsum('teh,ehd->ted', h, w2) + b2
        y = jnp.einsum('te,ted->td', rw, oe)
        z = _expert(xf, sw1, sb1, sw3, sb3, sw2, sb2)
        return (y + z).reshape(shape)
    x = L0_attn_x
    mod = (_silu(L0_c) @ L0_wmod).reshape(L0_c.shape[0], 6, 1, -1)
    sa, ca, ga, sb, cb, gb = (mod[:, 0], mod[:, 1], mod[:, 2], mod[:, 3], mod[:, 4], mod[:, 5])
    ga = (2 * (ga >= 0) - 1) * jnp.maximum(jnp.abs(ga), 0.25)
    gb = (2 * (gb >= 0) - 1) * jnp.maximum(jnp.abs(gb), 0.25)
    h = _layernorm(x, axis=-1) * (1 + ca) + sa
    x = x + ga * _L0_attn_ref(h, L0_attn_conv_w, L0_attn_conv_b, L0_attn_x_proj_dt_w, L0_attn_dt_proj_w, L0_attn_dt_proj_b, L0_attn_B_proj_w, L0_attn_C_proj_w, L0_attn_A_log, L0_attn_D_param)
    h = _layernorm(x, axis=-1) * (1 + cb) + sb
    x = x + gb * _L0_ffn_ref(h, L0_ffn_gate_w, L0_ffn_gate_b, L0_ffn_w1, L0_ffn_b1, L0_ffn_w3, L0_ffn_b3, L0_ffn_w2, L0_ffn_b2, L0_ffn_sw1, L0_ffn_sb1, L0_ffn_sw3, L0_ffn_sb3, L0_ffn_sw2, L0_ffn_sb2)
    return x

_drawn_inputs = setup_inputs


def setup_inputs(seed=0):
    import zlib

    import numpy as np

    out = dict(_drawn_inputs(seed))
    spreads = {'L0_attn_D_param': (1.0, 0.6)}
    factors = {'L0_attn_conv_b': 3.775,
     'L0_attn_x_proj_dt_w': 8.0,
     'L0_attn_dt_proj_w': 8.0,
     'L0_attn_dt_proj_b': 8.0,
     'L0_attn_B_proj_w': 8.0,
     'L0_attn_C_proj_w': 8.0,
     'L0_attn_A_log': 8.0,
     'L0_ffn_gate_w': 8.0,
     'L0_ffn_gate_b': 33.635,
     'L0_ffn_w1': 8.0,
     'L0_ffn_b1': 64.0,
     'L0_ffn_w3': 8.0,
     'L0_ffn_b3': 64.0,
     'L0_ffn_w2': 8.0,
     'L0_ffn_b2': 200.0,
     'L0_ffn_sw1': 8.0,
     'L0_ffn_sb1': 52.358,
     'L0_ffn_sw3': 8.0,
     'L0_ffn_sb3': 58.129,
     'L0_ffn_sw2': 8.0,
     'L0_ffn_sb2': 64.0}
    for name, (base, spread) in spreads.items():
        noise = np.random.default_rng([zlib.crc32(name.encode()), seed]).standard_normal(out[name].shape)
        drawn = base * np.exp(spread * noise) if base else spread * noise
        out[name] = jnp.asarray(drawn.astype(out[name].dtype))
    for name, factor in factors.items():
        out[name] = (out[name] * factor).astype(out[name].dtype)
    return out
```

```python
from contextlib import ExitStack

import concourse.bass as bass
from concourse import mybir

ALU = mybir.AluOpType
ACT = mybir.ActivationFunctionType
AX = mybir.AxisListType
F32 = mybir.dt.float32
BF16 = mybir.dt.bfloat16
U32 = mybir.dt.uint32

P = 128
CH = 512
SUB = CH // P
NB = 4
L = 1024
NCH = NB * L // CH
NS = 16
TAPS = 4
R = 64
E = 8
H = 176
HR = E * H
HA = HR + H
JR = HR // P
JA = -(-HA // P)
LAST = HA - (JA - 1) * P
EPS = 1e-5
HRING = 4
HP = 3
assert HR % P == 0


def width(j):
    return P if j < JA - 1 else LAST


class Chunk:

    def __init__(self, off, i=None, mult=0):
        self.off, self.i, self.mult = off, i, mult
        self.par = off % 2

    def plus(self, d):
        return Chunk(self.off + d, self.i, self.mult)

    def count(self, per, extra):
        v = self.off * per + extra
        return v if self.i is None else self.i * (self.mult * per) + v


EARLY = 6
SLOT_STATES = {1: 6, 3: 7, 5: 8, 7: 9, 9: 10, 11: 11, 13: 12}


def ring_order(scan, mix):
    out = [("N", n) for n in range(EARLY)] if scan else []
    for slot in range(JA + 1):
        if mix and 1 <= slot <= JR:
            out.append(("R", slot - 1))
        if scan and slot in SLOT_STATES:
            out.append(("N", SLOT_STATES[slot]))
    if scan:
        out += [("N", n) for n in range(13, NS)]
    return out


def ring_start(step):
    return 0 if step == 0 else NS + (NS + JR) * (step - 1)


def adaln_kernel(nc, x, conv_w, conv_b, xdt_w, dt_w, dt_b, b_w, c_w, a_log, d_par, gate_w, gate_b,
                 w1, b1, w3, b3, w2, b2, sw1, sb1, sw3, sb3, sw2, sb2, cond, wmod, out):
    x_tok = x.rearrange("b (k s p) d -> (b k) p s d", p=P, s=SUB)
    out_tok = out.rearrange("b (k s p) d -> (b k) p s d", p=P, s=SUB)
    c_dram = nc.dram_tensor("c_scratch", (2, NS, CH), F32).ap()

    with ExitStack() as ctx:
        def sb(name, shape, dt=F32):
            return ctx.enter_context(nc.sbuf_tensor(name, shape, dt))

        def bank(name, dt=F32):
            return ctx.enter_context(nc.psum_tensor(name, [P, CH], dt))

        def sem(name):
            return ctx.enter_context(nc.semaphore(name))

        w1_sb = sb("w1_sb", [P, HA])
        w3_sb = sb("w3_sb", [P, HA])
        w2_sb = sb("w2_sb", [P, JA, P])
        wmod_sb = sb("wmod_sb", [P, 6 * P])
        vec_rows = sb("vec_rows", [32, P])
        vec = sb("vec", [P, 32])
        B1, B3, CONVB, DPAR, DTB, SB2 = 0, JA, 2 * JA, 2 * JA + 1, 2 * JA + 2, 2 * JA + 3
        proj_rows = sb("proj_rows", [2 * NS + E, P])
        proj_t = sb("proj_t", [P, 2 * NS + E])
        bc_w = sb("bc_w", [P, 3, 2 * NS])
        cond_rows = sb("cond_rows", [NB, P])
        cond_act = sb("cond_act", [NB, P])
        cond_t = sb("cond_t", [P, NB])
        xdt_sb = sb("xdt_sb", [R, P])
        dt_rows = sb("dt_rows", [P, R])
        dt_t = sb("dt_t", [R, P])
        step_w = sb("step_w", [P, P])
        convw_sb = sb("convw_sb", [P, TAPS])
        alog_sb = sb("alog_sb", [P, NS])
        a_exp = sb("a_exp", [P, NS])
        a_neg = sb("a_neg", [P, NS])
        gateb_sb = sb("gateb_sb", [P, E])
        b2_rows = sb("b2_rows", [3 * E, P])
        b2_rest = sb("b2_rest", [3 * E, P])
        b2_part = sb("b2_part", [3 * E, 3, P], BF16)
        mod = sb("mod", [P, 6, NB])
        sign = sb("sign", [P, 2, NB])
        size = sb("size", [P, 2, NB])
        mods = sb("mods", [P, NB, 7])
        mod_prep = sb("mod_prep", [P, 2])
        mod_mix = sb("mod_mix", [P, 5])
        ident = sb("ident", [P, P])
        ident_b = sb("ident_b", [P, P], BF16)
        sel_state = sb("sel_state", [3 * 32, NS, P], BF16)
        sel_part = sb("sel_part", [3 * E, 3, JR * P], BF16)
        sel_expert = sb("sel_expert", [3 * E, JR, P], BF16)
        iota_f = sb("iota_f", [P, E])

        x_sb = sb("x_sb", [P, 2, SUB, P])
        stats = sb("stats", [P, 2, SUB, 6])
        mv = sb("mv", [P, 2, SUB, 2])
        lnv = sb("lnv", [P, 2, SUB])
        r0 = sb("r0", [P, 2, SUB])
        nt = sb("nt", [P, 2, 3, SUB])
        rstd = sb("rstd", [P, 2, SUB])
        xn = sb("xn", [P, 2, SUB, P])
        h_t = sb("h_t", [P, 2, TAPS - 1 + CH])
        cv = sb("cv", [P, 2, CH])
        xc = sb("xc", [P, 2, CH])
        z_abs = sb("z_abs", [P, CH])
        z_pos = sb("z_pos", [P, CH])
        e_neg = z_abs
        e_one = sb("e_one", [P, CH])
        l_one = sb("l_one", [P, CH])
        miss = sb("miss", [P, CH])
        soft = miss
        dt_sb = sb("dt_sb", [P, CH])
        u_sb = sb("u_sb", [P, 2, CH])
        b_split = sb("b_split", [96, 2, CH], BF16)
        b_rest = sb("b_rest", [96, CH])
        c_rows = sb("c_rows", [32, CH])
        c_all = sb("c_all", [P, NS, CH])
        decay = sb("decay", [P, NS, CH])
        h_s = sb("h_s", [P, HRING, CH])
        hc = sb("hc", [P, 2, CH])
        carry = sb("carry", [P, NS])
        acc = sb("acc", [P, 2, CH])
        y_d = sb("y_d", [P, CH])
        v_t = y_d
        x2 = sb("x2", [P, 2, CH])
        h2_t = sb("h2_t", [P, 2, CH])
        nmax = sb("nmax", [P, SUB])
        ls = sb("ls", [P, SUB, E])
        ge = sb("ge", [P, SUB, E])
        gsum = sb("gsum", [P, SUB])
        grec = sb("grec", [P, SUB])
        score = sb("score", [P, SUB, E])
        biased = sb("biased", [P, SUB, E])
        top = sb("top", [P, SUB, 8])
        topi = sb("topi", [P, SUB, 8], U32)
        topf = sb("topf", [P, SUB, 2])
        hot = sb("hot", [P, 2, SUB, E])
        rw = sb("rw", [P, SUB, E])
        rw_rest = sb("rw_rest", [P, SUB, E])
        rw_part = sb("rw_part", [P, SUB, 3, E], BF16)
        rw_t = sb("rw_t", [3 * E, CH], BF16)
        u3 = sb("u3", [P, 2, CH])
        z_sb = sb("z_sb", [P, 2, CH])
        s_sb = sb("s_sb", [P, 2, CH])
        hg = sb("hg", [P, HP, CH])
        v2 = sb("v2", [P, CH])
        o_sb = sb("o_sb", [P, 2, CH])

        bc_bank = [bank("bc0"), bank("bc1")]
        in_bank = [bank("in0"), bank("in1")]
        p3_bank = bank("p3_bank")
        p1_bank = bank("p1_bank")
        y_bank = bank("y_bank")
        misc = bank("misc")
        misc_t = misc[:, :].rearrange("p (s d) -> p s d", s=SUB)

        names = """w_in wr_in w2_in wm_in vz x_in ones_set id_set idb_set selz sel_s selp sel_e iota_set halo_set
        vecT vec_ready projT proj_ready bcw_ready cond_ready condT condt_ready dtT dtt_ready stepw_ps stepw_ready
        mod_ps mod_ready mod_a mod_b mods_ready aexp_ready aneg_ready b2_a b2_b b2_c b2_ready modp_set modm_set
        st1 mv1 lnv1 r1 nt1 rstd1 xn1 xnT1 ht_ready halo conv_step conv_ready xc_ready zdt_ready zdt_abs zdt_used
        eneg_ready eone_ready lone_ready miss_ready soft_ready dt_ready u_ready bcp_ready bhi_ready crow_ready
        brest_ready bmid_ready b_ready c_dram_in decay_ready
        bb_ready ub_done scan_done carry_done cmul acc_step acc_ready
        w_ready v_ready vT_ready x2_done st2 mv2 lnv2 r2 nt2 rstd2 xn2 xnT2 h2_ready lg_ready nmax_ready ls_ready
        ge_ready gsum_ready grec_ready score_ready biased_ready top_ready topi_ready topf_ready hot_ready hots_ready
        rw_ready rwh_ready rwr_ready rwm_ready r3_ready rwT_ready rwt_ready
        p3_ready u3_done p1_ready z_done s_done rwb_ready hg_done w2_done y_ready v2_ready v2T_ready out_ready
        st_out"""
        S = {n: sem(n) for n in names.split()}
        (w_in, wr_in, w2_in, wm_in, vz, x_in, ones_set, id_set, idb_set, selz, sel_s, selp, sel_e, iota_set,
         halo_set, vecT, vec_ready, projT, proj_ready, bcw_ready, cond_ready, condT, condt_ready, dtT, dtt_ready,
         stepw_ps, stepw_ready, mod_ps, mod_ready, mod_a, mod_b, mods_ready, aexp_ready, aneg_ready, b2_a, b2_b,
         b2_c, b2_ready, modp_set, modm_set, st1, mv1, lnv1, r1, nt1, rstd1, xn1, xnT1, ht_ready, halo, conv_step,
         conv_ready, xc_ready, zdt_ready, zdt_abs, zdt_used, eneg_ready, eone_ready, lone_ready, miss_ready,
         soft_ready, dt_ready, u_ready, bcp_ready, bhi_ready, crow_ready, brest_ready, bmid_ready, b_ready,
         c_dram_in, decay_ready, bb_ready, ub_done, scan_done, carry_done, cmul, acc_step, acc_ready, w_ready,
         v_ready, vT_ready, x2_done, st2, mv2, lnv2, r2, nt2, rstd2, xn2, xnT2, h2_ready, lg_ready, nmax_ready,
         ls_ready, ge_ready, gsum_ready, grec_ready, score_ready, biased_ready, top_ready, topi_ready, topf_ready,
         hot_ready, hots_ready, rw_ready, rwh_ready, rwr_ready, rwm_ready, r3_ready, rwT_ready, rwt_ready,
         p3_ready, u3_done, p1_ready, z_done, s_done, rwb_ready, hg_done, w2_done, y_ready, v2_ready, v2T_ready,
         out_ready, st_out) = S.values()
        c_in = [sem(f"c_in{g}") for g in range(4)]

        block = ctx.enter_context(nc.Block())

        def alone(eng):
            eng.nop(nofuse=True)

        def run(eng, step):
            step(0, Chunk(0), True, False, True)
            with eng.Fori(0, (NCH - 2) // 2) as i:
                step(1, Chunk(1, i, 2), True, True, True)
                step(2, Chunk(2, i, 2), True, True, True)
            step(NCH - 1, Chunk(NCH - 1), True, True, False)
            step(NCH, Chunk(NCH), False, True, False)

        @block.sync
        def _(sp):
            def rows(dst, src, s):
                sp.dma_start(dst, src).then_inc(s, 16)

            def one(v):
                return v.rearrange("(a n) -> a n", a=1)

            rows(x_sb[:, 0, :, :], x_tok[0], x_in)
            sp.wait_ge(vz, 1)
            rows(vec_rows[B1:B1 + JR, :], b1.rearrange("e h -> (e h)").rearrange("(k p) -> k p", p=P), wr_in)
            rows(vec_rows[B1 + JR:B1 + JR + 1, :], one(sb1)[:, 0:P], wr_in)
            rows(vec_rows[B1 + JR + 1:B1 + JA, 0:LAST], one(sb1)[:, P:H], wr_in)
            rows(vec_rows[B3:B3 + JR, :], b3.rearrange("e h -> (e h)").rearrange("(k p) -> k p", p=P), wr_in)
            rows(vec_rows[B3 + JR:B3 + JR + 1, :], one(sb3)[:, 0:P], wr_in)
            rows(vec_rows[B3 + JR + 1:B3 + JA, 0:LAST], one(sb3)[:, P:H], wr_in)
            rows(vec_rows[CONVB:CONVB + 1, :], one(conv_b), wr_in)
            rows(vec_rows[DPAR:DPAR + 1, :], one(d_par), wr_in)
            rows(vec_rows[DTB:DTB + 1, :], one(dt_b), wr_in)
            rows(vec_rows[SB2:SB2 + 1, :], one(sb2), wr_in)
            rows(w1_sb[:, 0:HR].rearrange("p (e h) -> p e h", e=E), w1.rearrange("e d h -> d e h"), w_in)
            rows(w1_sb[:, HR:HA], sw1, w_in)
            rows(w3_sb[:, 0:HR].rearrange("p (e h) -> p e h", e=E), w3.rearrange("e d h -> d e h"), w_in)
            rows(w3_sb[:, HR:HA], sw3, w_in)
            rows(w2_sb[:, 0:JR, :], w2.rearrange("e h d -> (e h) d").rearrange("(k p) d -> p k d", p=P), w2_in)
            rows(w2_sb[:, JR, :], sw2[0:P, :], w2_in)
            rows(w2_sb[0:LAST, JR + 1, :], sw2[P:H, :], w2_in)

            def load_x(k):
                if k.i is not None or k.off >= 2:
                    sp.wait_ge(x2_done, k.plus(-2).count(1, 1))
                    alone(sp)
                num = k.off if k.i is None else k.i * k.mult + k.off
                sp.dma_start(x_sb[:, k.par, :, :], x_tok[num]).then_inc(x_in, 16)

            def save_c(k):
                sp.wait_ge(crow_ready, k.count(1, 1))
                sp.dma_start(c_dram[k.par], c_rows[NS:2 * NS, :]).then_inc(c_dram_in, 16)
                sp.wait_ge(c_dram_in, k.count(16, 16))
                alone(sp)

            def spread_c(k, g):
                if k.i is not None or k.off:
                    sp.wait_ge(cmul, k.count(NS, 4 * g + 4 - NS))
                src = c_dram[k.par, 4 * g:4 * g + 4, :].rearrange("(a n) t -> a n t", a=1)
                sp.dma_start(c_all[:, 4 * g:4 * g + 4, :], src.broadcast_to([P, 4, CH])).then_inc(c_in[g], 16)

            def store(k):
                sp.wait_ge(out_ready, k.count(1, 1))
                alone(sp)
                num = k.off if k.i is None else k.i * k.mult + k.off
                sp.dma_start(out_tok[num], o_sb[:, k.par, :].rearrange("p (s d) -> p s d", s=SUB))\
                  .then_inc(st_out, 16)
                sp.wait_ge(st_out, k.count(16, 16))
                alone(sp)

            save_c(Chunk(0))
            for g in range(4):
                spread_c(Chunk(0), g)

            def step(number, c, scan, mix, prep):
                if prep:
                    load_x(c.plus(1))
                    save_c(c.plus(1))
                    for g in range(3):
                        spread_c(c.plus(1), g)
                if mix:
                    store(c.plus(-1))
                if prep:
                    spread_c(c.plus(1), 3)

            run(sp, step)

        @block.gpsimd
        def _(pool):
            pool.memset(ident[:, :], 0.0).then_inc(ones_set, 1)
            pool.memset(ident_b[:, :], 0.0).then_inc(ones_set, 1)
            pool.memset(sel_state[:, :, :], 0.0).then_inc(ones_set, 1)
            pool.memset(sel_part[:, :, :], 1.0).then_inc(ones_set, 1)
            pool.wait_ge(ones_set, 4)
            pool.affine_select(out=ident[:, :], in_=ident[:, :], compare_op=ALU.not_equal, fill=1.0, base=0,
                               pattern=[[-1, P]], channel_multiplier=1).then_inc(id_set, 1)
            pool.affine_select(out=ident_b[:, :], in_=ident_b[:, :], compare_op=ALU.not_equal, fill=1.0, base=0,
                               pattern=[[-1, P]], channel_multiplier=1).then_inc(idb_set, 1)
            for g in range(3):
                pool.affine_select(out=sel_state[:, :, :], in_=sel_state[:, :, :], compare_op=ALU.not_equal,
                                   fill=1.0, base=-32 * g, pattern=[[-1, NS], [0, P]], channel_multiplier=1)\
                    .then_inc(sel_s, 1)
                pool.wait_ge(sel_s, g + 1)
            for g in range(3):
                part = sel_part[:, g, :]
                pool.affine_select(out=part, in_=part, compare_op=ALU.is_ge, fill=0.0, base=H * E * g,
                                   pattern=[[1, JR * P]], channel_multiplier=-H).then_inc(selp, 1)
                pool.wait_ge(selp, 2 * g + 1)
                pool.affine_select(out=part, in_=part, compare_op=ALU.is_ge, fill=0.0, base=H - 1 - H * E * g,
                                   pattern=[[-1, JR * P]], channel_multiplier=H).then_inc(selp, 1)
                pool.wait_ge(selp, 2 * g + 2)
            flat = sel_expert[:, :, :].rearrange("r j m -> r (j m)")
            pool.tensor_tensor(flat, sel_part[:, 0, :], sel_part[:, 1, :], ALU.add).then_inc(sel_e, 1)
            pool.wait_ge(sel_e, 1)
            pool.tensor_tensor(flat, flat, sel_part[:, 2, :], ALU.add).then_inc(sel_e, 1)
            pool.iota(iota_f[:, :], [[1, E]], base=0, channel_multiplier=0,
                      allow_small_or_imprecise_dtypes=True).then_inc(iota_set, 1)

            def state(k, n):
                if n == 1 and (k.i is not None or k.off):
                    pool.wait_ge(acc_step, k.count(NS - 1, 0))
                pool.wait_ge(scan_done, k.count(NS, n + 1))
                if n % 4 == 0:
                    pool.wait_ge(c_in[n // 4], k.count(16, 16))
                h = h_s[:, n % HRING, :]
                if k.par == 0:
                    alone(pool)
                    pool.tensor_copy(carry[:, n:n + 1], h[:, CH - 1:CH]).then_inc(carry_done, 1)
                dst = acc[:, k.par, :] if n == 0 else hc[:, n % 2, :]
                if n >= 3:
                    pool.wait_ge(acc_step, k.count(NS - 1, n - 2))
                pool.tensor_tensor(dst, h, c_all[:, n, :], ALU.mult).then_inc(cmul, 1)

            def add(k, n):
                pool.wait_ge(cmul, k.count(NS, n + 1))
                if n >= 2:
                    pool.wait_ge(acc_step, k.count(NS - 1, n - 1))
                a = acc[:, k.par, :]
                pool.tensor_tensor(a, a, hc[:, n % 2, :], ALU.add).then_inc(acc_step, 1)

            def step(number, c, scan, mix, prep):
                if scan:
                    state(c, 0)
                    state(c, 1)
                    for n in range(2, NS):
                        state(c, n)
                        add(c, n - 1)
                    add(c, NS - 1)

            run(pool, step)

        @block.scalar
        def _(act):
            act.dma_start(proj_rows[0:NS, :], b_w).then_inc(wm_in, 16)
            act.dma_start(proj_rows[NS:2 * NS, :], c_w).then_inc(wm_in, 16)
            act.dma_start(proj_rows[2 * NS:2 * NS + E, :], gate_w).then_inc(wm_in, 16)
            act.dma_start(cond_rows[:, :], cond).then_inc(wm_in, 16)
            act.dma_start(xdt_sb[:, :], xdt_w).then_inc(wm_in, 16)
            act.dma_start(dt_rows[:, :], dt_w).then_inc(wm_in, 16)
            act.dma_start(convw_sb[:, :], conv_w.rearrange("d a t -> d (a t)")).then_inc(wm_in, 16)
            act.dma_start(alog_sb[:, :], a_log).then_inc(wm_in, 16)
            act.dma_start(gateb_sb[:, :], gate_b.rearrange("(a n) -> a n", a=1).broadcast_to([P, E]))\
               .then_inc(wm_in, 16)
            act.dma_start(wmod_sb[:, :], wmod).then_inc(wm_in, 16)
            for g in range(3):
                act.dma_start(b2_rows[E * g:E * g + E, :], b2).then_inc(wm_in, 16)
            act.wait_ge(wm_in, 16 * 13)
            act.activation(cond_act[:, :], cond_rows[:, :], ACT.Silu).then_inc(cond_ready, 1)
            act.activation(a_exp[:, :], alog_sb[:, :], ACT.Exp).then_inc(aexp_ready, 1)

            def rsqrt_start(k, which, mv_sem, l_sem, r_sem):
                act.wait_ge(mv_sem, k.count(1, 1))
                act.activation(lnv[:, which, :], mv[:, which, :, 1], ACT.Ln, bias=EPS).then_inc(l_sem, 1)
                act.wait_ge(l_sem, k.count(1, 1))
                act.activation(r0[:, which, :], lnv[:, which, :], ACT.Exp, scale=-0.5).then_inc(r_sem, 1)

            def modulate_prep(k):
                act.wait_ge(xnT1, k.count(1, 1))
                act.wait_ge(modp_set, (k.off // 2 + 1) if k.i is None else k.i + k.off // 2 + 1)
                act.activation(h_t[:, k.par, TAPS - 1:], misc[:, :], ACT.Identity, bias=mod_prep[:, 0:1],
                               scale=mod_prep[:, 1:2]).then_inc(ht_ready, 1)

            def conv_silu(k):
                act.wait_ge(conv_ready, k.count(1, 1))
                act.activation(xc[:, k.par, :], cv[:, 1, :], ACT.Silu, bias=vec[:, CONVB:CONVB + 1])\
                   .then_inc(xc_ready, 1)

            def softplus(k):
                bias = vec[:, DTB:DTB + 1]
                act.wait_ge(zdt_ready, k.count(1, 1))
                act.activation(z_abs[:, :], misc[:, :], ACT.Abs, bias=bias).then_inc(zdt_abs, 1)
                act.activation(z_pos[:, :], misc[:, :], ACT.Relu, bias=bias).then_inc(zdt_used, 1)
                act.wait_ge(zdt_abs, k.count(1, 1))
                act.activation(e_neg[:, :], z_abs[:, :], ACT.Exp, scale=-1.0).then_inc(eneg_ready, 1)
                act.wait_ge(eneg_ready, k.count(1, 1))
                act.activation(e_one[:, :], e_neg[:, :], ACT.Identity, bias=1.0).then_inc(eone_ready, 1)
                act.wait_ge(eone_ready, k.count(1, 1))
                act.activation(l_one[:, :], e_one[:, :], ACT.Ln).then_inc(lone_ready, 1)

            def split_b(k):
                act.wait_ge(bcp_ready, k.count(1, 1))
                act.activation(b_split[:, k.par, :], misc[0:96, :], ACT.Copy).then_inc(bhi_ready, 1)
                act.activation(c_rows[:, :], misc[0:32, :], ACT.Copy).then_inc(crow_ready, 1)
                act.wait_ge(brest_ready, k.count(1, 1))
                for lo, hi in ((32, 64), (64, 96)):
                    act.activation(b_split[lo:hi, k.par, :], b_rest[lo:hi, :], ACT.Copy).then_inc(bmid_ready, 1)

            def decays(k):
                act.wait_ge(dt_ready, k.count(1, 1))
                for n in range(NS):
                    if k.i is not None or k.off:
                        act.wait_ge(scan_done, k.count(NS, n + 1 - NS))
                    act.activation(decay[:, n, :], dt_sb[:, :], ACT.Exp, scale=a_neg[:, n:n + 1])\
                       .then_inc(decay_ready, 1)

            def u3_tile(k, j):
                m = width(j)
                act.wait_ge(p3_ready, k.count(JA, j + 1))
                if j >= 2:
                    act.wait_ge(z_done, k.count(JA, j - 1))
                act.activation(u3[0:m, j % 2, :], p3_bank[0:m, :], ACT.Identity, bias=vec[0:m, B3 + j:B3 + j + 1])\
                   .then_inc(u3_done, 1)

            def silu_tile(k, j):
                m = width(j)
                act.wait_ge(z_done, k.count(JA, j + 1))
                if j < JR:
                    dst = s_sb[0:m, j % 2, :]
                    if j >= 2:
                        act.wait_ge(hg_done, k.count(JR, j - 1))
                else:
                    dst = hg[0:m, j % HP, :]
                    act.wait_ge(w2_done, k.count(JA, j - HP + 1))
                act.activation(dst, z_sb[0:m, j % 2, :], ACT.Silu).then_inc(s_done, 1)

            act.wait_ge(aneg_ready, 1)
            rsqrt_start(Chunk(0), 0, mv1, lnv1, r1)
            modulate_prep(Chunk(0))
            conv_silu(Chunk(0))
            softplus(Chunk(0))
            split_b(Chunk(0))
            decays(Chunk(0))

            def step(number, c, scan, mix, prep):
                g, p = c.plus(-1), c.plus(1)
                if mix:
                    act.wait_ge(modm_set, (g.off // 2 + 1) if g.i is None else g.i + g.off // 2 + 1)
                    act.wait_ge(w_ready, g.count(1, 1))
                    act.activation(v_t[:, :], y_d[:, :], ACT.Identity, scale=mod_mix[:, 0:1]).then_inc(v_ready, 1)
                    rsqrt_start(g, 1, mv2, lnv2, r2)
                if prep:
                    rsqrt_start(p, 0, mv1, lnv1, r1)
                if mix:
                    act.wait_ge(xnT2, g.count(1, 1))
                    act.activation(h2_t[:, g.par, :], misc[:, :], ACT.Identity, bias=mod_mix[:, 1:2],
                                   scale=mod_mix[:, 2:3]).then_inc(h2_ready, 1)
                    act.wait_ge(ls_ready, g.count(1, 1))
                    act.activation(ge[:, :, :], ls[:, :, :], ACT.Exp).then_inc(ge_ready, 1)
                if prep:
                    modulate_prep(p)
                if mix:
                    act.wait_ge(rwT_ready, g.count(1, 1))
                    act.activation(rw_t[:, :], misc[0:3 * E, :], ACT.Copy).then_inc(rwt_ready, 1)
                    for slot in range(JA + 1):
                        if slot < JA:
                            u3_tile(g, slot)
                        if slot >= 1:
                            silu_tile(g, slot - 1)
                        if slot == 9 and prep:
                            conv_silu(p)
                elif prep:
                    conv_silu(p)
                if prep:
                    softplus(p)
                    split_b(p)
                if mix:
                    act.wait_ge(y_ready, g.count(1, 1))
                    act.activation(v2[:, :], y_bank[:, :], ACT.Identity, bias=mod_mix[:, 4:5],
                                   scale=mod_mix[:, 3:4]).then_inc(v2_ready, 1)
                if prep:
                    decays(p)

            run(act, step)

        @block.tensor
        def _(pe):
            pe.wait_ge(id_set, 1)
            pe.wait_ge(wm_in, 16 * 13)
            pe.transpose(misc[:, 0:2 * NS + E], proj_rows[:, :], ident[0:2 * NS + E, 0:2 * NS + E])\
              .then_inc(projT, 1)
            pe.transpose(p3_bank[0:R, 0:P], dt_rows[:, :], ident[:, :]).then_inc(dtT, 1)
            pe.wait_ge(cond_ready, 1)
            pe.transpose(in_bank[0][:, 0:NB], cond_act[:, :], ident[0:NB, 0:NB]).then_inc(condT, 1)
            pe.wait_ge(wr_in, 16 * 10)
            pe.transpose(bc_bank[0][:, 0:32], vec_rows[:, :], ident[0:32, 0:32]).then_inc(vecT, 1)
            pe.wait_ge(dtt_ready, 1)
            pe.matmul(y_bank[:, 0:P], xdt_sb[:, :], dt_t[:, :], start=True, stop=True).then_inc(stepw_ps, 1)
            pe.wait_ge(condt_ready, 1)
            for j in range(6):
                mm = pe.matmul(p1_bank[:, NB * j:NB * j + NB], wmod_sb[:, j * P:(j + 1) * P], cond_t[:, :],
                               start=True, stop=True)
            mm.then_inc(mod_ps, 1)
            pe.wait_ge(vec_ready, 1)
            pe.wait_ge(proj_ready, 1)
            pe.wait_ge(mod_ready, 1)
            pe.wait_ge(bcw_ready, 1)
            pe.wait_ge(stepw_ready, 1)

            def tok_to_feat(src):
                for s in range(SUB):
                    mm = pe.transpose(misc[:, s * P:(s + 1) * P], src[:, s, :], ident[:, :])
                return mm

            def feat_to_tok(src):
                for s in range(SUB):
                    mm = pe.transpose(misc[:, s * P:(s + 1) * P], src[:, s * P:(s + 1) * P], ident[:, :])
                return mm

            def step_sizes(k):
                pe.wait_ge(xc_ready, k.count(1, 1))
                pe.wait_ge(ht_ready, k.count(1, 1))
                pe.matmul(misc[:, :], step_w[:, :], xc[:, k.par, :], start=True, stop=True).then_inc(zdt_ready, 1)

            def bc_proj(k):
                pe.wait_ge(zdt_used, k.count(1, 1))
                pe.wait_ge(zdt_abs, k.count(1, 1))
                pe.matmul(misc[0:96, :], bc_w[:, :, :].rearrange("p a n -> p (a n)"), xc[:, k.par, :],
                          start=True, stop=True).then_inc(bcp_ready, 1)

            pe.wait_ge(xn1, 1)
            tok_to_feat(xn[:, 0, :, :]).then_inc(xnT1, 1)
            step_sizes(Chunk(0))
            bc_proj(Chunk(0))
            pe.wait_ge(sel_s, 3)

            def step(number, c, scan, mix, prep):
                g, p = c.plus(-1), c.plus(1)
                order = ring_order(scan, mix)
                start = ring_start(number)

                def ring(kind, n):
                    q = order.index((kind, n))
                    if q >= 2:
                        kind0, n0 = order[q - 2]
                        if kind0 == "N":
                            pe.wait_ge(ub_done, c.count(NS, n0 + 1))
                        else:
                            pe.wait_ge(hg_done, g.count(JR, n0 + 1))
                    elif number:
                        pe.wait_ge(ub_done, c.count(NS, q - 1))
                    return bc_bank[(start + q) % 2]

                def state(n):
                    if not scan:
                        return
                    to = ring("N", n)
                    if n == 0:
                        pe.wait_ge(b_ready, c.count(1, 1))
                    pe.matmul(to[:, :], sel_state[:, n, :], b_split[:, c.par, :], start=True, stop=True)\
                      .then_inc(bb_ready, 1)

                def weight(j):
                    pe.matmul(ring("R", j)[:, :], sel_expert[:, j, :], rw_t[:, :], start=True, stop=True)\
                      .then_inc(rwb_ready, 1)

                state(0)
                if mix:
                    pe.wait_ge(v_ready, g.count(1, 1))
                    feat_to_tok(v_t).then_inc(vT_ready, 1)
                state(1)
                state(2)
                state(3)
                if mix:
                    pe.wait_ge(xn2, g.count(1, 1))
                    pe.wait_ge(x2_done, g.count(1, 1))
                    tok_to_feat(xn[:, 1, :, :]).then_inc(xnT2, 1)
                    pe.wait_ge(h2_ready, g.count(1, 1))
                    for s in range(SUB):
                        mm = pe.matmul(misc[:, s * E:(s + 1) * E], h2_t[:, g.par, s * P:(s + 1) * P],
                                       proj_t[:, 2 * NS:2 * NS + E], start=True, stop=True)
                    mm.then_inc(lg_ready, 1)
                state(4)
                if prep:
                    if mix:
                        pe.wait_ge(ls_ready, g.count(1, 1))
                    pe.wait_ge(xn1, p.count(1, 1))
                    if not mix:
                        pe.wait_ge(brest_ready, p.count(1, 0))
                        pe.wait_ge(crow_ready, p.count(1, 0))
                    tok_to_feat(xn[:, 0, :, :]).then_inc(xnT1, 1)
                state(5)
                if mix:
                    pe.wait_ge(r3_ready, g.count(1, 1))
                    if prep:
                        pe.wait_ge(ht_ready, p.count(1, 1))
                    for s in range(SUB):
                        mm = pe.matmul(misc[0:3 * E, s * P:(s + 1) * P],
                                       rw_part[:, s, :, :].rearrange("p a e -> p (a e)"), ident_b[:, :],
                                       start=True, stop=True)
                    mm.then_inc(rwT_ready, 1)
                    if number == 1:
                        pe.wait_ge(w_in, 16 * 4)
                        pe.wait_ge(w2_in, 16 * 3)
                        pe.wait_ge(sel_e, 2)
                        pe.wait_ge(b2_ready, 1)
                    for slot in range(JA + 2):
                        j = slot
                        if j < JA:
                            m = width(j)
                            if j:
                                pe.wait_ge(u3_done, g.count(JA, j))
                            pe.matmul(p3_bank[0:m, :], w3_sb[:, j * P:j * P + m], h2_t[:, g.par, :],
                                      start=True, stop=True).then_inc(p3_ready, 1)
                            if j:
                                pe.wait_ge(z_done, g.count(JA, j))
                            pe.matmul(p1_bank[0:m, :], w1_sb[:, j * P:j * P + m], h2_t[:, g.par, :],
                                      start=True, stop=True).then_inc(p1_ready, 1)
                        if 1 <= slot <= JR:
                            if slot == 1:
                                pe.wait_ge(rwt_ready, g.count(1, 1))
                            weight(slot - 1)
                        if slot in SLOT_STATES:
                            state(SLOT_STATES[slot])
                        j = slot - 2
                        if j >= 0:
                            m = width(j)
                            if j < JR:
                                pe.wait_ge(hg_done, g.count(JR, j + 1))
                            else:
                                pe.wait_ge(s_done, g.count(JA, j + 1))
                            pe.matmul(y_bank[:, :], w2_sb[0:m, j, :], hg[0:m, j % HP, :], start=(j == 0),
                                      stop=False).then_inc(w2_done, 1)
                    for q in range(3):
                        mm = pe.matmul(y_bank[:, :], b2_part[:, q, :], rw_t[:, :], start=False, stop=(q == 2))
                    mm.then_inc(y_ready, 1)
                else:
                    for slot in sorted(SLOT_STATES):
                        state(SLOT_STATES[slot])
                if prep:
                    if mix:
                        pe.wait_ge(rwt_ready, g.count(1, 1))
                    step_sizes(p)
                state(13)
                if prep:
                    bc_proj(p)
                state(14)
                state(15)
                if mix:
                    pe.wait_ge(v2_ready, g.count(1, 1))
                    if prep:
                        pe.wait_ge(brest_ready, p.count(1, 1))
                        pe.wait_ge(crow_ready, p.count(1, 1))
                    feat_to_tok(v2).then_inc(v2T_ready, 1)

            run(pe, step)

        @block.vector
        def _(dve):
            dve.memset(vec_rows[:, :], 0.0).then_inc(vz, 1)
            dve.memset(h_t[:, 0, 0:TAPS - 1], 0.0).then_inc(halo_set, 1)
            dve.wait_ge(projT, 1)
            dve.tensor_copy(proj_t[:, :], misc[:, 0:2 * NS + E]).then_inc(proj_ready, 1)
            dve.wait_ge(dtT, 1)
            dve.tensor_copy(dt_t[:, :], p3_bank[0:R, 0:P]).then_inc(dtt_ready, 1)
            dve.wait_ge(condT, 1)
            dve.tensor_copy(cond_t[:, :], in_bank[0][:, 0:NB]).then_inc(condt_ready, 1)
            dve.wait_ge(vecT, 1)
            dve.tensor_copy(vec[:, :], bc_bank[0][:, 0:32]).then_inc(vec_ready, 1)
            dve.wait_ge(proj_ready, 1)
            for a in range(3):
                cp = dve.tensor_copy(bc_w[:, a, :], proj_t[:, 0:2 * NS])
            cp.then_inc(bcw_ready, 1)
            dve.wait_ge(stepw_ps, 1)
            dve.tensor_copy(step_w[:, :], y_bank[:, 0:P]).then_inc(stepw_ready, 1)
            dve.wait_ge(aexp_ready, 1)
            dve.tensor_scalar(a_neg[:, :], a_exp[:, :], -1.0, None, ALU.mult).then_inc(aneg_ready, 1)
            dve.wait_ge(mod_ps, 1)
            dve.tensor_copy(mod[:, :, :].rearrange("p j b -> p (j b)"), p1_bank[:, 0:6 * NB]).then_inc(mod_ready, 1)
            dve.wait_ge(mod_ready, 1)
            for a, j in enumerate((2, 5)):
                dve.tensor_scalar(sign[:, a, :], mod[:, j, :], 0.0, 2.0, ALU.is_ge, ALU.mult).then_inc(mod_a, 1)
                dve.wait_ge(mod_a, 3 * a + 1)
                dve.scalar_tensor_tensor(size[:, a, :], sign[:, a, :], -1.0, mod[:, j, :], ALU.add, ALU.mult)\
                   .then_inc(mod_a, 1)
                dve.wait_ge(mod_a, 3 * a + 2)
                dve.tensor_scalar(size[:, a, :], size[:, a, :], 0.25, None, ALU.max).then_inc(mod_a, 1)
            dve.wait_ge(mod_a, 6)
            dve.tensor_copy(mods[:, :, 0], mod[:, 0, :])
            dve.tensor_scalar(mods[:, :, 1], mod[:, 1, :], 1.0, None, ALU.add)
            dve.scalar_tensor_tensor(mods[:, :, 2], sign[:, 0, :], -1.0, size[:, 0, :], ALU.add, ALU.mult)
            dve.tensor_copy(mods[:, :, 3], mod[:, 3, :])
            dve.tensor_scalar(mods[:, :, 4], mod[:, 4, :], 1.0, None, ALU.add)
            dve.scalar_tensor_tensor(mods[:, :, 5], sign[:, 1, :], -1.0, size[:, 1, :], ALU.add, ALU.mult)\
               .then_inc(mod_b, 1)
            dve.wait_ge(mod_b, 1)
            dve.wait_ge(vec_ready, 1)
            dve.tensor_scalar(mods[:, :, 6], mods[:, :, 5], vec[:, SB2:SB2 + 1], None, ALU.mult)\
               .then_inc(mods_ready, 1)
            dve.wait_ge(mods_ready, 1)
            dve.tensor_copy(mod_prep[:, :], mods[:, 0, 0:2]).then_inc(modp_set, 1)
            dve.wait_ge(wm_in, 16 * 13)
            dve.tensor_copy(b2_part[:, 0, :], b2_rows[:, :]).then_inc(b2_a, 1)
            dve.wait_ge(b2_a, 1)
            dve.tensor_tensor(b2_rest[:, :], b2_rows[:, :], b2_part[:, 0, :], ALU.subtract).then_inc(b2_b, 1)
            dve.wait_ge(b2_b, 1)
            dve.tensor_copy(b2_part[:, 1, :], b2_rest[:, :]).then_inc(b2_c, 1)
            dve.wait_ge(b2_c, 1)
            dve.tensor_tensor(b2_part[:, 2, :], b2_rest[:, :], b2_part[:, 1, :], ALU.subtract).then_inc(b2_ready, 1)
            dve.wait_ge(iota_set, 1)

            def moments(k, which, src, s_stats, s_mv):
                for s in range(SUB):
                    st = dve.bn_stats(stats[:, which, s, :], src[:, s, :])
                st.then_inc(s_stats, 1)
                dve.wait_ge(s_stats, k.count(1, 1))
                alone(dve)
                for s in range(SUB):
                    ag = dve.bn_aggr(mv[:, which, s, :], stats[:, which, s, :])
                ag.then_inc(s_mv, 1)

            def normalise(k, which, src, s_r, s_nt, s_rstd, s_xn):
                dve.wait_ge(s_r, k.count(1, 1))
                t = nt[:, which, :, :]
                dve.tensor_tensor(t[:, 0, :], r0[:, which, :], r0[:, which, :], ALU.mult).then_inc(s_nt, 1)
                dve.wait_ge(s_nt, k.count(3, 1))
                dve.scalar_tensor_tensor(t[:, 1, :], mv[:, which, :, 1], EPS, t[:, 0, :], ALU.add, ALU.mult)\
                   .then_inc(s_nt, 1)
                dve.wait_ge(s_nt, k.count(3, 2))
                dve.tensor_scalar(t[:, 2, :], t[:, 1, :], -0.5, 1.5, ALU.mult, ALU.add).then_inc(s_nt, 1)
                dve.wait_ge(s_nt, k.count(3, 3))
                dve.tensor_tensor(rstd[:, which, :], r0[:, which, :], t[:, 2, :], ALU.mult).then_inc(s_rstd, 1)
                dve.wait_ge(s_rstd, k.count(1, 1))
                for s in range(SUB):
                    ts = dve.tensor_scalar(xn[:, which, s, :], src[:, s, :], mv[:, which, s, 0:1],
                                           rstd[:, which, s:s + 1], ALU.subtract, ALU.mult)
                ts.then_inc(s_xn, 1)

            def prep_moments(k):
                dve.wait_ge(x_in, k.count(16, 16))
                moments(k, 0, x_sb[:, k.par, :, :], st1, mv1)

            def prep_normalise(k):
                normalise(k, 0, x_sb[:, k.par, :, :], r1, nt1, rstd1, xn1)

            def convolve(k):
                dve.wait_ge(ht_ready, k.count(1, 1))
                h = h_t[:, k.par, :]
                if k.par == 1:
                    dve.tensor_copy(h[:, 0:TAPS - 1], h_t[:, 0, CH:CH + TAPS - 1]).then_inc(halo, 1)
                    dve.wait_ge(halo, (k.off // 2 + 1) if k.i is None else k.i + k.off // 2 + 1)
                dve.tensor_scalar(cv[:, 0, :], h[:, 0:CH], convw_sb[:, 0:1], None, ALU.mult).then_inc(conv_step, 1)
                for t in range(1, TAPS):
                    dve.wait_ge(conv_step, k.count(3, t))
                    dve.scalar_tensor_tensor(cv[:, t % 2, :], h[:, t:t + CH], convw_sb[:, t:t + 1],
                                             cv[:, (t - 1) % 2, :], ALU.mult, ALU.add)\
                       .then_inc(conv_step if t < TAPS - 1 else conv_ready, 1)

            def step_size(k):
                dve.wait_ge(eone_ready, k.count(1, 1))
                dve.scalar_tensor_tensor(miss[:, :], e_one[:, :], 1.0, e_neg[:, :], ALU.subtract, ALU.subtract)\
                   .then_inc(miss_ready, 1)
                dve.wait_ge(miss_ready, k.count(1, 1))
                dve.wait_ge(lone_ready, k.count(1, 1))
                dve.tensor_tensor(soft[:, :], l_one[:, :], miss[:, :], ALU.subtract).then_inc(soft_ready, 1)
                dve.wait_ge(soft_ready, k.count(1, 1))
                dve.tensor_tensor(dt_sb[:, :], soft[:, :], z_pos[:, :], ALU.add).then_inc(dt_ready, 1)

            def scan_input(k):
                dve.wait_ge(dt_ready, k.count(1, 1))
                dve.tensor_tensor(u_sb[:, k.par, :], dt_sb[:, :], xc[:, k.par, :], ALU.mult).then_inc(u_ready, 1)

            def b_remainder(k):
                dve.wait_ge(bhi_ready, k.count(1, 1))
                dve.wait_ge(crow_ready, k.count(1, 1))
                dve.tensor_tensor(b_rest[:, :], misc[0:96, :], b_split[:, k.par, :], ALU.subtract)\
                   .then_inc(brest_ready, 1)

            def b_low(k):
                dve.wait_ge(bmid_ready, k.count(2, 2))
                low = b_split[64:96, k.par, :]
                dve.tensor_tensor(low, b_rest[64:96, :], low, ALU.subtract).then_inc(b_ready, 1)

            prep_moments(Chunk(0))
            prep_normalise(Chunk(0))
            convolve(Chunk(0))
            step_size(Chunk(0))
            scan_input(Chunk(0))
            b_remainder(Chunk(0))
            b_low(Chunk(0))

            def step(number, c, scan, mix, prep):
                g, p = c.plus(-1), c.plus(1)
                order = ring_order(scan, mix)
                start = ring_start(number)

                def spread(kind, n):
                    return bc_bank[(start + order.index((kind, n))) % 2]

                def scan_state(n):
                    dve.wait_ge(ub_done, c.count(NS, n + 1))
                    dve.wait_ge(decay_ready, c.count(NS, n + 1))
                    if n >= HRING:
                        dve.wait_ge(cmul, c.count(NS, n - HRING + 1))
                    first = 0.0
                    if c.par == 1:
                        dve.wait_ge(carry_done, (c.off // 2 * NS + n + 1) if c.i is None
                                    else c.i * NS + (c.off // 2 * NS + n + 1))
                        first = carry[:, n:n + 1]
                    dve.tensor_tensor_scan(h_s[:, n % HRING, :], decay[:, n, :], in_bank[n % 2][:, :],
                                           first, ALU.mult, ALU.add).then_inc(scan_done, 1)

                def state(n):
                    if not scan:
                        return
                    if n == 0:
                        dve.wait_ge(u_ready, c.count(1, 1))
                    dve.wait_ge(bb_ready, c.count(NS, n + 1))
                    if n >= 2 or number:
                        dve.wait_ge(scan_done, c.count(NS, n - 1))
                    dve.tensor_tensor(in_bank[n % 2][:, :], u_sb[:, c.par, :], spread("N", n)[:, :], ALU.mult)\
                       .then_inc(ub_done, 1)
                    if n >= 1:
                        scan_state(n - 1)

                if number % 2 == 1 and mix:
                    b = g.off // 2 if g.i is None else g.i + g.off // 2
                    dve.tensor_copy(mod_mix[:, :], mods[:, b, 2:7]).then_inc(modm_set, 1)
                    if prep:
                        b = p.off // 2 if p.i is None else p.i + p.off // 2
                        dve.tensor_copy(mod_prep[:, :], mods[:, b, 0:2]).then_inc(modp_set, 1)
                if mix:
                    dve.wait_ge(acc_step, g.count(NS - 1, NS - 1))
                    dve.scalar_tensor_tensor(y_d[:, :], xc[:, g.par, :], vec[:, DPAR:DPAR + 1], acc[:, g.par, :],
                                             ALU.mult, ALU.add).then_inc(w_ready, 1)
                state(0)
                x2_tok = x2[:, g.par, :].rearrange("p (s d) -> p s d", s=SUB)
                if mix:
                    dve.wait_ge(vT_ready, g.count(1, 1))
                    dve.tensor_tensor(x2_tok, misc_t, x_sb[:, g.par, :, :], ALU.add).then_inc(x2_done, 1)
                state(1)
                if mix:
                    dve.wait_ge(x2_done, g.count(1, 1))
                    moments(g, 1, x2_tok, st2, mv2)
                if prep:
                    prep_moments(p)
                state(2)
                if mix:
                    normalise(g, 1, x2_tok, r2, nt2, rstd2, xn2)
                state(3)
                if prep:
                    prep_normalise(p)
                if mix:
                    logits = misc[:, 0:SUB * E].rearrange("p (s e) -> p s e", s=SUB)
                    dve.wait_ge(lg_ready, g.count(1, 1))
                    dve.tensor_reduce(nmax[:, :], logits, AX.X, ALU.max, negate=True).then_inc(nmax_ready, 1)
                    dve.wait_ge(nmax_ready, g.count(1, 1))
                    dve.tensor_tensor(ls[:, :, :], logits, nmax[:, :].unsqueeze(2).broadcast_to([P, SUB, E]),
                                      ALU.add).then_inc(ls_ready, 1)
                state(4)
                if mix:
                    dve.wait_ge(ge_ready, g.count(1, 1))
                    dve.tensor_reduce(gsum[:, :], ge[:, :, :], AX.X, ALU.add).then_inc(gsum_ready, 1)
                    dve.wait_ge(gsum_ready, g.count(1, 1))
                    dve.reciprocal(grec[:, :], gsum[:, :]).then_inc(grec_ready, 1)
                    dve.wait_ge(grec_ready, g.count(1, 1))
                    dve.tensor_tensor(score[:, :, :], ge[:, :, :], grec[:, :].unsqueeze(2).broadcast_to([P, SUB, E]),
                                      ALU.mult).then_inc(score_ready, 1)
                    dve.wait_ge(score_ready, g.count(1, 1))
                    dve.tensor_tensor(biased[:, :, :], score[:, :, :],
                                      gateb_sb[:, :].unsqueeze(1).broadcast_to([P, SUB, E]), ALU.add)\
                       .then_inc(biased_ready, 1)
                    dve.wait_ge(biased_ready, g.count(1, 1))
                    alone(dve)
                    for s in range(SUB):
                        mx = dve.max(top[:, s, :], biased[:, s, :])
                    mx.then_inc(top_ready, 1)
                    dve.wait_ge(top_ready, g.count(1, 1))
                    alone(dve)
                    for s in range(SUB):
                        mx = dve.max_index(topi[:, s, :], top[:, s, :], biased[:, s, :])
                    mx.then_inc(topi_ready, 1)
                    dve.wait_ge(topi_ready, g.count(1, 1))
                    dve.tensor_copy(topf[:, :, :], topi[:, :, 0:2]).then_inc(topf_ready, 1)
                    dve.wait_ge(topf_ready, g.count(1, 1))
                    for a in range(2):
                        eq = dve.tensor_tensor(hot[:, a, :, :], iota_f[:, :].unsqueeze(1).broadcast_to([P, SUB, E]),
                                               topf[:, :, a:a + 1].broadcast_to([P, SUB, E]), ALU.is_equal)
                    eq.then_inc(hot_ready, 1)
                    dve.wait_ge(hot_ready, g.count(1, 1))
                    dve.tensor_tensor(hot[:, 0, :, :], hot[:, 0, :, :], hot[:, 1, :, :], ALU.add)\
                       .then_inc(hots_ready, 1)
                    dve.wait_ge(hots_ready, g.count(1, 1))
                    dve.tensor_tensor(rw[:, :, :], score[:, :, :], hot[:, 0, :, :], ALU.mult).then_inc(rw_ready, 1)
                    dve.wait_ge(rw_ready, g.count(1, 1))
                    dve.tensor_copy(rw_part[:, :, 0, :], rw[:, :, :]).then_inc(rwh_ready, 1)
                    dve.wait_ge(rwh_ready, g.count(1, 1))
                    dve.tensor_tensor(rw_rest[:, :, :], rw[:, :, :], rw_part[:, :, 0, :], ALU.subtract)\
                       .then_inc(rwr_ready, 1)
                    dve.wait_ge(rwr_ready, g.count(1, 1))
                    dve.tensor_copy(rw_part[:, :, 1, :], rw_rest[:, :, :]).then_inc(rwm_ready, 1)
                    dve.wait_ge(rwm_ready, g.count(1, 1))
                    dve.tensor_tensor(rw_part[:, :, 2, :], rw_rest[:, :, :], rw_part[:, :, 1, :], ALU.subtract)\
                       .then_inc(r3_ready, 1)
                state(5)
                if mix:
                    for slot in range(JA + 1):
                        j = slot
                        if j < JA:
                            m = width(j)
                            dve.wait_ge(u3_done, g.count(JA, j + 1))
                            dve.wait_ge(p1_ready, g.count(JA, j + 1))
                            if j >= 2:
                                dve.wait_ge(s_done, g.count(JA, j - 1))
                            dve.scalar_tensor_tensor(z_sb[0:m, j % 2, :], p1_bank[0:m, :],
                                                     vec[0:m, B1 + j:B1 + j + 1], u3[0:m, j % 2, :],
                                                     ALU.add, ALU.mult).then_inc(z_done, 1)
                        j = slot - 1
                        if 0 <= j < JR:
                            dve.wait_ge(s_done, g.count(JA, j + 1))
                            dve.wait_ge(rwb_ready, g.count(JR, j + 1))
                            if j >= HP:
                                dve.wait_ge(w2_done, g.count(JA, j - HP + 1))
                            dve.tensor_tensor(hg[:, j % HP, :], s_sb[:, j % 2, :], spread("R", j)[:, :],
                                              ALU.mult).then_inc(hg_done, 1)
                        if slot in SLOT_STATES:
                            state(SLOT_STATES[slot])
                        if slot == 5 and prep:
                            convolve(p)
                else:
                    for slot in sorted(SLOT_STATES):
                        state(SLOT_STATES[slot])
                        if slot == 5 and prep:
                            convolve(p)
                if prep:
                    step_size(p)
                state(13)
                if prep:
                    scan_input(p)
                state(14)
                if prep:
                    b_remainder(p)
                state(15)
                if prep:
                    b_low(p)
                if scan:
                    scan_state(NS - 1)
                if mix:
                    dve.wait_ge(v2T_ready, g.count(1, 1))
                    if number == NCH:
                        dve.wait_ge(st_out, 16 * (NCH - 2))
                    dve.tensor_tensor(o_sb[:, g.par, :].rearrange("p (s d) -> p s d", s=SUB), misc_t, x2_tok,
                                      ALU.add).then_inc(out_ready, 1)

            run(dve, step)


_INS = ['L0_attn_x', 'L0_attn_conv_w', 'L0_attn_conv_b', 'L0_attn_x_proj_dt_w', 'L0_attn_dt_proj_w',
        'L0_attn_dt_proj_b', 'L0_attn_B_proj_w', 'L0_attn_C_proj_w', 'L0_attn_A_log', 'L0_attn_D_param',
        'L0_ffn_gate_w', 'L0_ffn_gate_b', 'L0_ffn_w1', 'L0_ffn_b1', 'L0_ffn_w3', 'L0_ffn_b3', 'L0_ffn_w2',
        'L0_ffn_b2', 'L0_ffn_sw1', 'L0_ffn_sb1', 'L0_ffn_sw3', 'L0_ffn_sb3', 'L0_ffn_sw2', 'L0_ffn_sb2',
        'L0_c', 'L0_wmod']
_OUTS = [((4, 1024, 128), 'float32')]


def kernel(**inputs):
    import numpy as _np
    import concourse.bacc as _bacc
    from concourse import mybir as _mybir
    from concourse.bass_utils import run_bass_kernel_spmd as _run

    nc = _bacc.Bacc("TRN2", target_bir_lowering=False, num_devices=1)
    arrays, args = {}, []
    for name in _INS:
        a = _np.ascontiguousarray(inputs[name])
        arrays[f"in_{name}_dram"] = a
        args.append(nc.dram_tensor(f"in_{name}_dram", a.shape, _mybir.dt.from_np(a.dtype), kind="ExternalInput").ap())
    for i, (shape, dtype) in enumerate(_OUTS):
        dt = _mybir.dt.from_np(_np.dtype(dtype))
        args.append(nc.dram_tensor(f"out_{i}_dram", shape, dt, kind="ExternalOutput").ap())
    adaln_kernel(nc, *args)
    r = _run(nc, [arrays], core_ids=[0])
    got = tuple(r.results[0][f"out_{i}_dram"] for i in range(len(_OUTS)))
    return got[0]
```

```python
from contextlib import ExitStack

import concourse.bass as bass
from concourse import mybir

ALU = mybir.AluOpType
ACT = mybir.ActivationFunctionType
AX = mybir.AxisListType
F32 = mybir.dt.float32
BF16 = mybir.dt.bfloat16
U32 = mybir.dt.uint32
F32R = mybir.dt.float32r
HIGH_BITS = 0xFFFFF000

P = 128
CH = 512
SUB = CH // P
NB = 4
L = 1024
NCH = NB * L // CH
NS = 16
TAPS = 4
R = 64
E = 8
H = 176
HR = E * H
HA = HR + H
JR = HR // P
JA = -(-HA // P)
LAST = HA - (JA - 1) * P
EPS = 1e-5
HRING = 4
HP = 3
assert HR % P == 0


def width(j):
    return P if j < JA - 1 else LAST


class Chunk:

    def __init__(self, off, i=None, mult=0):
        self.off, self.i, self.mult = off, i, mult
        self.par = off % 2

    def plus(self, d):
        return Chunk(self.off + d, self.i, self.mult)

    def count(self, per, extra):
        v = self.off * per + extra
        return v if self.i is None else self.i * (self.mult * per) + v


EARLY = 6
SLOT_STATES = {1: 6, 2: 7, 4: 8, 6: 9, 8: 10, 9: 11, 10: 12, 11: 13, 12: 14, 13: 15}
LATE = EARLY + len(SLOT_STATES)
DECAYS_0, DECAYS_1, DECAYS_2, DECAYS_3 = 4, 4, 10, 14
AT_HT, AT_CONV, AT_SILU, AT_ENDS, AT_SPLIT, AT_MID, AT_SOFT = 2, 2, 6, 8, 8, 9, 9


def ring_order(scan, mix):
    out = [("N", n) for n in range(EARLY)] if scan else []
    for slot in range(1, JA + 1):
        if mix and slot <= JR:
            out.append(("R", slot - 1))
        if scan and slot in SLOT_STATES:
            out.append(("N", SLOT_STATES[slot]))
    if scan:
        out += [("N", n) for n in range(LATE, NS)]
    return out


def ring_start(step):
    return 0 if step == 0 else NS + (NS + JR) * (step - 1)


def adaln_kernel(nc, x, conv_w, conv_b, xdt_w, dt_w, dt_b, b_w, c_w, a_log, d_par, gate_w, gate_b,
                 w1, b1, w3, b3, w2, b2, sw1, sb1, sw3, sb3, sw2, sb2, cond, wmod, out):
    x_tok = x.rearrange("b (k s p) d -> (b k) p s d", p=P, s=SUB)
    out_tok = out.rearrange("b (k s p) d -> (b k) p s d", p=P, s=SUB)
    c_dram = nc.dram_tensor("c_scratch", (2, NS, CH), F32).ap()

    with ExitStack() as ctx:
        def sb(name, shape, dt=F32):
            return ctx.enter_context(nc.sbuf_tensor(name, shape, dt))

        def bank(name, dt=F32):
            return ctx.enter_context(nc.psum_tensor(name, [P, CH], dt))

        def sem(name):
            return ctx.enter_context(nc.semaphore(name))

        w1_hi = sb("w1_hi", [P, HA], F32R)
        w1_lo = sb("w1_lo", [P, HA], F32R)
        w3_hi = sb("w3_hi", [P, HA], F32R)
        w3_lo = sb("w3_lo", [P, HA], F32R)
        w2_sb = sb("w2_sb", [P, JA, P])
        vec_rows = sb("vec_rows", [32, P])
        vec = sb("vec", [P, 32])
        B1, B3, CONVB, DPAR, DTB, SB2 = 0, JA, 2 * JA, 2 * JA + 1, 2 * JA + 2, 2 * JA + 3
        proj_rows = sb("proj_rows", [2 * NS + E, P])
        proj_t = sb("proj_t", [P, 2 * NS + E])
        bc_w = sb("bc_w", [P, 3, 2 * NS])
        cond_rows = sb("cond_rows", [NB, P])
        cond_act = sb("cond_act", [NB, P])
        cond_t = sb("cond_t", [P, NB])
        xdt_sb = sb("xdt_sb", [R, P])
        dt_rows = sb("dt_rows", [P, R])
        dt_t = sb("dt_t", [R, P])
        step_w = sb("step_w", [P, P])
        convw_sb = sb("convw_sb", [P, TAPS])
        alog_sb = sb("alog_sb", [P, NS])
        a_exp = sb("a_exp", [P, NS])
        a_neg = sb("a_neg", [P, NS])
        gateb_sb = sb("gateb_sb", [P, E])
        b2_rows = sb("b2_rows", [3 * E, P])
        b2_rest = sb("b2_rest", [3 * E, P])
        b2_part = sb("b2_part", [3 * E, 3, P], BF16)
        mod = sb("mod", [P, 6, NB])
        sign = sb("sign", [P, 2, NB])
        size = sb("size", [P, 2, NB])
        mods = sb("mods", [P, NB, 8])
        mod_prep = sb("mod_prep", [P, 2])
        mod_mix = sb("mod_mix", [P, 4])
        mod_gate = sb("mod_gate", [P, 2])
        gate_diag = sb("gate_diag", [P, 2, P])
        probe = sb("probe", [P, 1])
        ident = sb("ident", [P, P])
        ident_b = sb("ident_b", [P, P], BF16)
        sel_state = sb("sel_state", [3 * 32, NS, P], BF16)
        sel_expert = sb("sel_expert", [3 * E, JR, P], BF16)
        iota_f = sb("iota_f", [P, E])

        x_sb = sb("x_sb", [P, 2, SUB, P])
        stats = sb("stats", [P, 2, SUB, 6])
        mv = sb("mv", [P, 2, SUB, 2])
        ve = sb("ve", [P, 2, SUB])
        half = sb("half", [P, SUB])
        r0 = sb("r0", [P, 2, SUB])
        nt = sb("nt", [P, 2, 2, SUB])
        rstd = sb("rstd", [P, 2, SUB])
        xn = sb("xn", [P, 2, SUB, P])
        h_t = sb("h_t", [P, 2, TAPS - 1 + CH])
        cv = sb("cv", [P, 2, CH])
        xc = sb("xc", [P, 2, CH])
        z_abs = sb("z_abs", [P, CH])
        z_pos = sb("z_pos", [P, CH])
        e_neg = z_abs
        e_one = sb("e_one", [P, CH])
        l_one = sb("l_one", [P, CH])
        miss = sb("miss", [P, CH])
        dt_sb = sb("dt_sb", [P, CH])
        u_sb = sb("u_sb", [P, 2, CH])
        b_split = sb("b_split", [96, 2, CH], BF16)
        b_rest = sb("b_rest", [96, CH])
        c_rows = sb("c_rows", [32, CH])
        c_all = sb("c_all", [P, NS, CH])
        decay = sb("decay", [P, NS, CH])
        wmod_sb = decay[:, 14:16, :].rearrange("p n t -> p (n t)")[:, 0:6 * P]
        sel_part = decay[0:3 * E, 8:13, :].rearrange("p n t -> p (n t)").bitcast(BF16)[:, 0:3 * JR * P]\
            .rearrange("p (g f) -> p g f", g=3)
        h_s = sb("h_s", [P, HRING, CH])
        hc = sb("hc", [P, 2, CH])
        carry = sb("carry", [P, NS])
        acc = sb("acc", [P, 2, CH])
        mix_work = sb("mix_work", [P, 11 + HP, CH])
        x2, o_sb = mix_work[:, 0:2, :], mix_work[:, 2:4, :]
        v2 = mix_work[:, 4, :]
        u3, z_sb, s_sb = mix_work[:, 5:7, :], mix_work[:, 7:9, :], mix_work[:, 9:11, :]
        hg = mix_work[:, 11:, :]
        h2_m = v2
        w_flat = mix_work[:, :, :].rearrange("p n t -> p (n t)")
        w1_all, w3_all = w_flat[:, 0:HA], w_flat[:, HA:2 * HA]
        w1_m, w3_m = w_flat[:, 2 * HA:3 * HA], w_flat[:, 3 * HA:4 * HA]
        assert 4 * HA <= (11 + HP) * CH
        h2_t = sb("h2_t", [P, CH])
        h2_hi = sb("h2_hi", [P, CH], F32R)
        h2_lo = sb("h2_lo", [P, CH], F32R)
        nmax = sb("nmax", [P, SUB])
        ls = sb("ls", [P, SUB, E])
        ge = sb("ge", [P, SUB, E])
        gsum = sb("gsum", [P, SUB])
        grec = sb("grec", [P, SUB])
        score = sb("score", [P, SUB, E])
        biased = sb("biased", [P, SUB, E])
        top = sb("top", [P, SUB, 8])
        topi = sb("topi", [P, SUB, 8], U32)
        topf = sb("topf", [P, SUB, 2])
        hot = sb("hot", [P, 2, SUB, E])
        rw = sb("rw", [P, SUB, E])
        rw_rest = sb("rw_rest", [P, SUB, E])
        rw_part = sb("rw_part", [P, SUB, 3, E], BF16)
        rw_t = sb("rw_t", [3 * E, CH], BF16)

        bc_bank = [bank("bc0"), bank("bc1")]
        in_bank = [bank("in0"), bank("in1")]
        p3_bank = bank("p3_bank")
        p1_bank = bank("p1_bank")
        y_bank = bank("y_bank")
        misc = bank("misc")
        misc_t = misc[:, :].rearrange("p (s d) -> p s d", s=SUB)

        names = """w_in wr_in w2_in wm_in vz x_in ones_set id_set idb_set selz sel_s selp sel_e iota_set halo_set
        vecT vec_ready projT proj_ready bcw_ready cond_ready condT condt_ready dtT dtt_ready stepw_ps stepw_ready
        mod_ps mod_ready mod_a mod_b mods_ready aexp_ready aneg_ready b2_a b2_b b2_c b2_ready modp_set modm_set modg_set
        st1 mv1 ve1 r1 nt1 rstd1 xn1 xnT1 ht_ready halo conv_step conv_ready xc_ready zdt_ready zdt_abs zdt_used
        eneg_ready eone_ready lone_ready lzero_ready miss_ready dt_ready u_ready bcp_ready bhi_ready crow_ready
        brest_ready bmid_ready b_ready c_dram_in decay_ready
        bb_ready ub_done scan_done carry_done cmul acc_step acc_ready
        x2_ready x2_done diag_set mods_b st2 mv2 ve2 r2 nt2 rstd2 xn2 xnT2 h2_ready hh_ready h2s_ready whi_ready wsplit_ready half_set base_ready lg_ready nmax_ready ls_ready
        ge_ready gsum_ready grec_ready score_ready biased_ready top_ready topi_ready topf_ready hot_ready hots_ready
        rw_ready rwh_ready rwr_ready rwm_ready r3_ready rwT_ready rwt_ready
        p3_ready u3_done p1_ready z_done s_done rwb_ready hg_done w2_done v2_ready out_ps out_ready
        st_out"""
        S = {n: sem(n) for n in names.split()}
        (w_in, wr_in, w2_in, wm_in, vz, x_in, ones_set, id_set, idb_set, selz, sel_s, selp, sel_e, iota_set,
         halo_set, vecT, vec_ready, projT, proj_ready, bcw_ready, cond_ready, condT, condt_ready, dtT, dtt_ready,
         stepw_ps, stepw_ready, mod_ps, mod_ready, mod_a, mod_b, mods_ready, aexp_ready, aneg_ready, b2_a, b2_b,
         b2_c, b2_ready, modp_set, modm_set, modg_set, st1, mv1, ve1, r1, nt1, rstd1, xn1, xnT1, ht_ready, halo, conv_step,
         conv_ready, xc_ready, zdt_ready, zdt_abs, zdt_used, eneg_ready, eone_ready, lone_ready, lzero_ready, miss_ready,
         dt_ready, u_ready, bcp_ready, bhi_ready, crow_ready, brest_ready, bmid_ready, b_ready,
         c_dram_in, decay_ready, bb_ready, ub_done, scan_done, carry_done, cmul, acc_step, acc_ready, 
         x2_ready, x2_done, diag_set, mods_b, st2, mv2, ve2, r2, nt2, rstd2, xn2, xnT2, h2_ready, hh_ready, h2s_ready, whi_ready, wsplit_ready, half_set, base_ready, lg_ready, nmax_ready,
         ls_ready, ge_ready, gsum_ready, grec_ready, score_ready, biased_ready, top_ready, topi_ready, topf_ready,
         hot_ready, hots_ready, rw_ready, rwh_ready, rwr_ready, rwm_ready, r3_ready, rwT_ready, rwt_ready,
         p3_ready, u3_done, p1_ready, z_done, s_done, rwb_ready, hg_done, w2_done, v2_ready, out_ps,
         out_ready, st_out) = S.values()
        c_in = [sem(f"c_in{g}") for g in range(4)]

        block = ctx.enter_context(nc.Block())

        def alone(eng):
            eng.nop(nofuse=True)

        def run(eng, step):
            step(0, Chunk(0), True, False, True)
            with eng.Fori(0, (NCH - 2) // 2) as i:
                step(1, Chunk(1, i, 2), True, True, True)
                step(2, Chunk(2, i, 2), True, True, True)
            step(NCH - 1, Chunk(NCH - 1), True, True, False)
            step(NCH, Chunk(NCH), False, True, False)

        @block.sync
        def _(sp):
            def rows(dst, src, s):
                sp.dma_start(dst, src).then_inc(s, 16)

            def one(v):
                return v.rearrange("(a n) -> a n", a=1)

            rows(x_sb[:, 0, :, :], x_tok[0], x_in)
            sp.wait_ge(vz, 1)
            rows(vec_rows[B1:B1 + JR, :], b1.rearrange("e h -> (e h)").rearrange("(k p) -> k p", p=P), wr_in)
            rows(vec_rows[B1 + JR:B1 + JR + 1, :], one(sb1)[:, 0:P], wr_in)
            rows(vec_rows[B1 + JR + 1:B1 + JA, 0:LAST], one(sb1)[:, P:H], wr_in)
            rows(vec_rows[B3:B3 + JR, :], b3.rearrange("e h -> (e h)").rearrange("(k p) -> k p", p=P), wr_in)
            rows(vec_rows[B3 + JR:B3 + JR + 1, :], one(sb3)[:, 0:P], wr_in)
            rows(vec_rows[B3 + JR + 1:B3 + JA, 0:LAST], one(sb3)[:, P:H], wr_in)
            rows(vec_rows[CONVB:CONVB + 1, :], one(conv_b), wr_in)
            rows(vec_rows[DPAR:DPAR + 1, :], one(d_par), wr_in)
            rows(vec_rows[DTB:DTB + 1, :], one(dt_b), wr_in)
            rows(vec_rows[SB2:SB2 + 1, :], one(sb2), wr_in)
            rows(w1_all[:, 0:HR].rearrange("p (e h) -> p e h", e=E), w1.rearrange("e d h -> d e h"), w_in)
            rows(w1_all[:, HR:HA], sw1, w_in)
            rows(w3_all[:, 0:HR].rearrange("p (e h) -> p e h", e=E), w3.rearrange("e d h -> d e h"), w_in)
            rows(w3_all[:, HR:HA], sw3, w_in)
            rows(w2_sb[:, 0:JR, :], w2.rearrange("e h d -> (e h) d").rearrange("(k p) d -> p k d", p=P), w2_in)
            rows(w2_sb[:, JR, :], sw2[0:P, :], w2_in)
            rows(w2_sb[0:LAST, JR + 1, :], sw2[P:H, :], w2_in)

            def load_x(k):
                if k.i is not None or k.off >= 2:
                    sp.wait_ge(x2_ready, k.plus(-2).count(1, 1))
                    alone(sp)
                num = k.off if k.i is None else k.i * k.mult + k.off
                sp.dma_start(x_sb[:, k.par, :, :], x_tok[num]).then_inc(x_in, 16)

            def save_c(k):
                sp.wait_ge(crow_ready, k.count(1, 1))
                sp.dma_start(c_dram[k.par], c_rows[NS:2 * NS, :]).then_inc(c_dram_in, 16)
                sp.wait_ge(c_dram_in, k.count(16, 16))
                alone(sp)

            def spread_c(k, g):
                if k.i is not None or k.off:
                    sp.wait_ge(cmul, k.count(NS, 4 * g + 4 - NS))
                src = c_dram[k.par, 4 * g:4 * g + 4, :].rearrange("(a n) t -> a n t", a=1)
                sp.dma_start(c_all[:, 4 * g:4 * g + 4, :], src.broadcast_to([P, 4, CH])).then_inc(c_in[g], 16)

            def store(k):
                sp.wait_ge(out_ready, k.count(1, 2))
                alone(sp)
                num = k.off if k.i is None else k.i * k.mult + k.off
                sp.dma_start(out_tok[num], o_sb[:, k.par, :].rearrange("p (s d) -> p s d", s=SUB))\
                  .then_inc(st_out, 16)
                sp.wait_ge(st_out, k.count(16, 16))
                alone(sp)

            save_c(Chunk(0))
            for g in range(4):
                spread_c(Chunk(0), g)

            def step(number, c, scan, mix, prep):
                if prep:
                    load_x(c.plus(1))
                    save_c(c.plus(1))
                    for g in range(3):
                        spread_c(c.plus(1), g)
                if mix:
                    store(c.plus(-1))
                if prep:
                    spread_c(c.plus(1), 3)

            run(sp, step)

        @block.gpsimd
        def _(pool):
            pool.memset(ident[:, :], 0.0).then_inc(ones_set, 1)
            pool.memset(ident_b[:, :], 0.0).then_inc(ones_set, 1)
            pool.memset(sel_state[:, :, :], 0.0).then_inc(ones_set, 1)
            pool.memset(sel_part[:, :, :], 1.0).then_inc(ones_set, 1)
            pool.wait_ge(ones_set, 4)
            pool.affine_select(out=ident[:, :], in_=ident[:, :], compare_op=ALU.not_equal, fill=1.0, base=0,
                               pattern=[[-1, P]], channel_multiplier=1).then_inc(id_set, 1)
            pool.affine_select(out=ident_b[:, :], in_=ident_b[:, :], compare_op=ALU.not_equal, fill=1.0, base=0,
                               pattern=[[-1, P]], channel_multiplier=1).then_inc(idb_set, 1)
            for g in range(3):
                pool.affine_select(out=sel_state[:, :, :], in_=sel_state[:, :, :], compare_op=ALU.not_equal,
                                   fill=1.0, base=-32 * g, pattern=[[-1, NS], [0, P]], channel_multiplier=1)\
                    .then_inc(sel_s, 1)
                pool.wait_ge(sel_s, g + 1)
            for g in range(3):
                part = sel_part[:, g, :]
                pool.affine_select(out=part, in_=part, compare_op=ALU.is_ge, fill=0.0, base=H * E * g,
                                   pattern=[[1, JR * P]], channel_multiplier=-H).then_inc(selp, 1)
                pool.wait_ge(selp, 2 * g + 1)
                pool.affine_select(out=part, in_=part, compare_op=ALU.is_ge, fill=0.0, base=H - 1 - H * E * g,
                                   pattern=[[-1, JR * P]], channel_multiplier=H).then_inc(selp, 1)
                pool.wait_ge(selp, 2 * g + 2)
            flat = sel_expert[:, :, :].rearrange("r j m -> r (j m)")
            pool.tensor_tensor(flat, sel_part[:, 0, :], sel_part[:, 1, :], ALU.add).then_inc(sel_e, 1)
            pool.wait_ge(sel_e, 1)
            pool.tensor_tensor(flat, flat, sel_part[:, 2, :], ALU.add).then_inc(sel_e, 1)
            pool.memset(half[:, :], -0.5).then_inc(half_set, 1)
            pool.iota(iota_f[:, :], [[1, E]], base=0, channel_multiplier=0,
                      allow_small_or_imprecise_dtypes=True).then_inc(iota_set, 1)

            def state(k, n):
                if n == 1 and (k.i is not None or k.off):
                    pool.wait_ge(acc_step, k.count(NS - 1, 0))
                pool.wait_ge(scan_done, k.count(NS, n + 1))
                if n % 4 == 0:
                    pool.wait_ge(c_in[n // 4], k.count(16, 16))
                h = h_s[:, n % HRING, :]
                if k.par == 0:
                    alone(pool)
                    pool.tensor_copy(carry[:, n:n + 1], h[:, CH - 1:CH]).then_inc(carry_done, 1)
                dst = acc[:, k.par, :] if n == 0 else hc[:, n % 2, :]
                if n >= 3:
                    pool.wait_ge(acc_step, k.count(NS - 1, n - 2))
                pool.tensor_tensor(dst, h, c_all[:, n, :], ALU.mult).then_inc(cmul, 1)

            def add(k, n):
                pool.wait_ge(cmul, k.count(NS, n + 1))
                if n >= 2:
                    pool.wait_ge(acc_step, k.count(NS - 1, n - 1))
                a = acc[:, k.par, :]
                pool.tensor_tensor(a, a, hc[:, n % 2, :], ALU.add).then_inc(acc_step, 1)

            def rsqrt_start(k, which, ve_sem, r_sem):
                pool.wait_ge(ve_sem, k.count(1, 1))
                pool.tensor_tensor(r0[:, which, :], ve[:, which, :], half[:, :], ALU.pow).then_inc(r_sem, 1)

            pool.wait_ge(half_set, 1)
            rsqrt_start(Chunk(0), 0, ve1, r1)

            def step(number, c, scan, mix, prep):
                if scan:
                    state(c, 0)
                if mix:
                    rsqrt_start(c.plus(-1), 1, ve2, r2)
                if scan:
                    state(c, 1)
                    for n in range(2, NS):
                        state(c, n)
                        add(c, n - 1)
                        if n == 2 and prep:
                            rsqrt_start(c.plus(1), 0, ve1, r1)
                    add(c, NS - 1)

            run(pool, step)

        @block.scalar
        def _(act):
            act.dma_start(proj_rows[0:NS, :], b_w).then_inc(wm_in, 16)
            act.dma_start(proj_rows[NS:2 * NS, :], c_w).then_inc(wm_in, 16)
            act.dma_start(proj_rows[2 * NS:2 * NS + E, :], gate_w).then_inc(wm_in, 16)
            act.dma_start(cond_rows[:, :], cond).then_inc(wm_in, 16)
            act.dma_start(xdt_sb[:, :], xdt_w).then_inc(wm_in, 16)
            act.dma_start(dt_rows[:, :], dt_w).then_inc(wm_in, 16)
            act.dma_start(convw_sb[:, :], conv_w.rearrange("d a t -> d (a t)")).then_inc(wm_in, 16)
            act.dma_start(alog_sb[:, :], a_log).then_inc(wm_in, 16)
            act.dma_start(gateb_sb[:, :], gate_b.rearrange("(a n) -> a n", a=1).broadcast_to([P, E]))\
               .then_inc(wm_in, 16)
            act.dma_start(wmod_sb[:, :], wmod).then_inc(wm_in, 16)
            for g in range(3):
                act.dma_start(b2_rows[E * g:E * g + E, :], b2).then_inc(wm_in, 16)
            act.wait_ge(wm_in, 16 * 13)
            act.activation(cond_act[:, :], cond_rows[:, :], ACT.Silu).then_inc(cond_ready, 1)
            act.activation(a_exp[:, :], alog_sb[:, :], ACT.Exp).then_inc(aexp_ready, 1)

            def load_table(func):
                return act.activation(probe[:, :], some, func)

            def modulate_prep(k):
                act.wait_ge(xnT1, k.count(1, 1))
                act.wait_ge(modp_set, (k.off // 2 + 1) if k.i is None else k.i + k.off // 2 + 1)
                act.activation(h_t[:, k.par, TAPS - 1:], misc[:, :], ACT.Identity, bias=mod_prep[:, 0:1],
                               scale=mod_prep[:, 1:2]).then_inc(ht_ready, 1)

            def conv_silu(k):
                act.wait_ge(conv_ready, k.count(1, 1))
                act.activation(xc[:, k.par, :], cv[:, 1, :], ACT.Silu, bias=vec[:, CONVB:CONVB + 1])\
                   .then_inc(xc_ready, 1)

            def softplus_ends(k):
                bias = vec[:, DTB:DTB + 1]
                act.wait_ge(zdt_ready, k.count(1, 1))
                act.activation(z_abs[:, :], misc[:, :], ACT.Abs, bias=bias).then_inc(zdt_abs, 1)
                act.activation(z_pos[:, :], misc[:, :], ACT.Relu, bias=bias).then_inc(zdt_used, 1)

            def softplus(k):
                act.wait_ge(zdt_abs, k.count(1, 1))
                act.activation(e_neg[:, :], z_abs[:, :], ACT.Exp, scale=-1.0).then_inc(eneg_ready, 1)
                act.wait_ge(eneg_ready, k.count(1, 1))
                act.activation(e_one[:, :], e_neg[:, :], ACT.Identity, bias=1.0).then_inc(eone_ready, 1)
                act.wait_ge(eone_ready, k.count(1, 1))
                act.activation(l_one[:, :], e_one[:, :], ACT.Ln).then_inc(lone_ready, 1)

            def split_high(k):
                act.wait_ge(bcp_ready, k.count(1, 1))
                act.activation(b_split[:, k.par, :], misc[0:96, :], ACT.Copy).then_inc(bhi_ready, 1)
                act.activation(c_rows[:, :], misc[0:32, :], ACT.Copy).then_inc(crow_ready, 1)

            def split_mid(k):
                act.wait_ge(brest_ready, k.count(1, 1))
                for lo, hi in ((32, 64), (64, 96)):
                    act.activation(b_split[lo:hi, k.par, :], b_rest[lo:hi, :], ACT.Copy).then_inc(bmid_ready, 1)

            def decays(k, first, end):
                if first == 0:
                    act.wait_ge(dt_ready, k.count(1, 1))
                    if k.i is None and k.off == 0:
                        act.wait_ge(mod_ps, 1)
                        act.wait_ge(sel_e, 2)
                for n in range(first, end):
                    if k.i is not None or k.off:
                        act.wait_ge(scan_done, k.count(NS, n + 1 - NS))
                    act.activation(decay[:, n, :], dt_sb[:, :], ACT.Exp, scale=a_neg[:, n:n + 1])\
                       .then_inc(decay_ready, 1)

            def u3_tile(k, j):
                m = width(j)
                act.wait_ge(p3_ready, k.count(JA, j + 1))
                if j >= 2:
                    act.wait_ge(z_done, k.count(JA, j - 1))
                act.activation(u3[0:m, j % 2, :], p3_bank[0:m, :], ACT.Identity, bias=vec[0:m, B3 + j:B3 + j + 1])\
                   .then_inc(u3_done, 1)

            def silu_tile(k, j):
                m = width(j)
                act.wait_ge(z_done, k.count(JA, j + 1))
                if j < JR:
                    dst = s_sb[0:m, j % 2, :]
                    if j >= 2:
                        act.wait_ge(hg_done, k.count(JR, j - 1))
                else:
                    dst = hg[0:m, j % HP, :]
                    act.wait_ge(w2_done, k.count(JA, j - HP + 1))
                act.activation(dst, z_sb[0:m, j % 2, :], ACT.Silu).then_inc(s_done, 1)

            act.wait_ge(aneg_ready, 1)
            some = vec[:, 0:1]
            act.wait_ge(vec_ready, 1)
            modulate_prep(Chunk(0))
            conv_silu(Chunk(0))
            softplus_ends(Chunk(0))
            split_high(Chunk(0))
            split_mid(Chunk(0))
            softplus(Chunk(0))

            def step(number, c, scan, mix, prep):
                g, p = c.plus(-1), c.plus(1)
                if scan:
                    decays(c, DECAYS_0 if number else 0, DECAYS_1)
                if mix:
                    act.wait_ge(x2_ready, g.count(1, 1))
                    act.wait_ge(st2, g.count(1, 1))
                    act.activation(x2[:, g.par, :], misc[:, :], ACT.Copy).then_inc(x2_done, 1)
                if scan:
                    decays(c, DECAYS_1, DECAYS_2)
                if mix:
                    act.wait_ge(modm_set, (g.off // 2 + 1) if g.i is None else g.i + g.off // 2 + 1)
                    act.wait_ge(xnT2, g.count(1, 1))
                    act.activation(h2_t[:, :], misc[:, :], ACT.Identity, bias=mod_mix[:, 0:1],
                                   scale=mod_mix[:, 1:2]).then_inc(h2_ready, 1)
                if scan:
                    decays(c, DECAYS_2, DECAYS_3)
                if mix:
                    act.wait_ge(ls_ready, g.count(1, 1))
                    act.activation(ge[:, :, :], ls[:, :, :], ACT.Exp).then_inc(ge_ready, 1)
                if scan:
                    decays(c, DECAYS_3, NS)
                load_table(ACT.Silu)
                if mix:
                    u3_tile(g, 0)
                    u3_tile(g, 1)
                    silu_tile(g, 0)
                    act.wait_ge(rwT_ready, g.count(1, 1))
                    act.activation(rw_t[:, :], misc[0:3 * E, :], ACT.Copy).then_inc(rwt_ready, 1)
                    for slot in range(2, JA + 1):
                        if slot < JA:
                            u3_tile(g, slot)
                        silu_tile(g, slot - 1)
                        if prep:
                            if slot == AT_HT:
                                modulate_prep(p)
                            if slot == AT_SILU:
                                conv_silu(p)
                            if slot == AT_ENDS:
                                softplus_ends(p)
                            if slot == AT_SPLIT:
                                split_high(p)
                            if slot == AT_SOFT:
                                softplus(p)
                            if slot == AT_MID:
                                split_mid(p)
                elif prep:
                    modulate_prep(p)
                    conv_silu(p)
                    softplus_ends(p)
                    split_high(p)
                    split_mid(p)
                    softplus(p)
                if mix:
                    act.wait_ge(w2_done, g.count(JA, JA))
                    act.activation(v2, y_bank[:, :], ACT.Identity, bias=mod_mix[:, 3:4],
                                   scale=mod_mix[:, 2:3]).then_inc(v2_ready, 1)
                if number == 0:
                    load_table(ACT.Exp).then_inc(out_ready, 1)
                if prep:
                    decays(p, 0, DECAYS_0)
                if mix:
                    act.wait_ge(out_ps, g.count(1, 1))
                    if number == NCH:
                        act.wait_ge(st_out, 16 * (NCH - 2))
                    act.activation(o_sb[:, g.par, :], misc[:, :], ACT.Copy).then_inc(out_ready, 1)

            run(act, step)

        @block.tensor
        def _(pe):
            pe.wait_ge(id_set, 1)
            pe.wait_ge(wm_in, 16 * 13)
            pe.transpose(misc[:, 0:2 * NS + E], proj_rows[:, :], ident[0:2 * NS + E, 0:2 * NS + E])\
              .then_inc(projT, 1)
            pe.transpose(p3_bank[0:R, 0:P], dt_rows[:, :], ident[:, :]).then_inc(dtT, 1)
            pe.wait_ge(cond_ready, 1)
            pe.transpose(in_bank[0][:, 0:NB], cond_act[:, :], ident[0:NB, 0:NB]).then_inc(condT, 1)
            pe.wait_ge(wr_in, 16 * 10)
            pe.transpose(bc_bank[0][:, 0:32], vec_rows[:, :], ident[0:32, 0:32]).then_inc(vecT, 1)
            pe.wait_ge(dtt_ready, 1)
            pe.matmul(y_bank[:, 0:P], xdt_sb[:, :], dt_t[:, :], start=True, stop=True).then_inc(stepw_ps, 1)
            pe.wait_ge(condt_ready, 1)
            for j in range(6):
                mm = pe.matmul(p1_bank[:, NB * j:NB * j + NB], wmod_sb[:, j * P:(j + 1) * P], cond_t[:, :],
                               start=True, stop=True)
            mm.then_inc(mod_ps, 1)
            pe.wait_ge(vec_ready, 1)
            pe.wait_ge(proj_ready, 1)
            pe.wait_ge(mod_ready, 1)
            pe.wait_ge(bcw_ready, 1)
            pe.wait_ge(stepw_ready, 1)

            def tok_to_feat(src):
                for s in range(SUB):
                    mm = pe.transpose(misc[:, s * P:(s + 1) * P], src[:, s, :], ident[:, :])
                return mm

            def add_transposed(src, diag, last):
                for s in range(SUB):
                    mm = pe.matmul(misc[:, s * P:(s + 1) * P], src[:, s * P:(s + 1) * P], diag,
                                   start=False, stop=last and s == SUB - 1)
                return mm

            def step_sizes(k):
                pe.wait_ge(xc_ready, k.count(1, 1))
                pe.wait_ge(ht_ready, k.count(1, 1))
                pe.matmul(misc[:, :], step_w[:, :], xc[:, k.par, :], start=True, stop=True).then_inc(zdt_ready, 1)

            def bc_proj(k):
                pe.wait_ge(zdt_used, k.count(1, 1))
                pe.wait_ge(zdt_abs, k.count(1, 1))
                pe.matmul(misc[0:96, :], bc_w[:, :, :].rearrange("p a n -> p (a n)"), xc[:, k.par, :],
                          start=True, stop=True).then_inc(bcp_ready, 1)

            pe.wait_ge(xn1, 1)
            tok_to_feat(xn[:, 0, :, :]).then_inc(xnT1, 1)
            step_sizes(Chunk(0))
            bc_proj(Chunk(0))
            pe.wait_ge(sel_s, 3)

            def step(number, c, scan, mix, prep):
                g, p = c.plus(-1), c.plus(1)
                order = ring_order(scan, mix)
                start = ring_start(number)

                def ring(kind, n):
                    q = order.index((kind, n))
                    if q >= 2:
                        kind0, n0 = order[q - 2]
                        if kind0 == "N":
                            pe.wait_ge(ub_done, c.count(NS, n0 + 1))
                        else:
                            pe.wait_ge(hg_done, g.count(JR, n0 + 1))
                    elif number:
                        pe.wait_ge(ub_done, c.count(NS, q - 1))
                    return bc_bank[(start + q) % 2]

                def state(n):
                    if not scan:
                        return
                    to = ring("N", n)
                    if n == 0:
                        pe.wait_ge(b_ready, c.count(1, 1))
                    pe.matmul(to[:, :], sel_state[:, n, :], b_split[:, c.par, :], start=True, stop=True)\
                      .then_inc(bb_ready, 1)

                def weight(j):
                    pe.matmul(ring("R", j)[:, :], sel_expert[:, j, :], rw_t[:, :], start=True, stop=True)\
                      .then_inc(rwb_ready, 1)

                def experts_in(j):
                    m = width(j)
                    if j == 0:
                        pe.wait_ge(h2s_ready, g.count(1, 1))
                    else:
                        pe.wait_ge(u3_done, g.count(JA, j))
                    for hi, lo, to, done in ((w3_hi, w3_lo, p3_bank, p3_ready), (w1_hi, w1_lo, p1_bank, p1_ready)):
                        if j and done is p1_ready:
                            pe.wait_ge(z_done, g.count(JA, j))
                        cols = slice(j * P, j * P + m)
                        pe.matmul(to[0:m, :], hi[:, cols], h2_hi[:, :], start=True, stop=False)
                        pe.matmul(to[0:m, :], hi[:, cols], h2_lo[:, :], start=False, stop=False)
                        pe.matmul(to[0:m, :], lo[:, cols], h2_hi[:, :], start=False, stop=True).then_inc(done, 1)

                def experts_out(j):
                    m = width(j)
                    if j < JR:
                        pe.wait_ge(hg_done, g.count(JR, j + 1))
                    else:
                        pe.wait_ge(s_done, g.count(JA, j + 1))
                    pe.matmul(y_bank[:, :], w2_sb[0:m, j, :], hg[0:m, j % HP, :], start=(j == 0),
                              stop=(j == JA - 1)).then_inc(w2_done, 1)

                def prep_transpose():
                    pe.wait_ge(xn1, p.count(1, 1))
                    if mix:
                        pe.wait_ge(rwt_ready, g.count(1, 1))
                    else:
                        pe.wait_ge(brest_ready, p.count(1, 0))
                        pe.wait_ge(crow_ready, p.count(1, 0))
                    tok_to_feat(xn[:, 0, :, :]).then_inc(xnT1, 1)

                state(0)
                state(1)
                if mix:
                    pe.wait_ge(diag_set, (g.off // 2 + 1) if g.i is None else g.i + g.off // 2 + 1)
                    pe.wait_ge(out_ready, g.count(1, 1))
                    pe.matmul(misc[:, :], ident[:, :], x_sb[:, g.par, :, :].rearrange("p s d -> p (s d)"),
                              start=True, stop=False)
                    add_transposed(xc[:, g.par, :], gate_diag[:, 1, :], False)
                    pe.wait_ge(acc_step, g.count(NS - 1, NS - 1))
                    add_transposed(acc[:, g.par, :], gate_diag[:, 0, :], True).then_inc(x2_ready, 1)
                state(2)
                state(3)
                if mix:
                    pe.wait_ge(xn2, g.count(1, 1))
                    pe.wait_ge(x2_done, g.count(1, 1))
                    tok_to_feat(xn[:, 1, :, :]).then_inc(xnT2, 1)
                    pe.wait_ge(h2_ready, g.count(1, 1))
                    for s in range(SUB):
                        mm = pe.matmul(misc[:, s * E:(s + 1) * E], h2_t[:, s * P:(s + 1) * P],
                                       proj_t[:, 2 * NS:2 * NS + E], start=True, stop=True)
                    mm.then_inc(lg_ready, 1)
                for n in range(4, EARLY):
                    state(n)
                if mix:
                    if number == 1:
                        pe.wait_ge(wsplit_ready, 2)
                        pe.wait_ge(w2_in, 16 * 3)
                        pe.wait_ge(sel_e, 2)
                        pe.wait_ge(b2_ready, 1)
                    experts_in(0)
                    experts_in(1)
                    pe.wait_ge(r3_ready, g.count(1, 1))
                    for s in range(SUB):
                        mm = pe.matmul(misc[0:3 * E, s * P:(s + 1) * P],
                                       rw_part[:, s, :, :].rearrange("p a e -> p (a e)"), ident_b[:, :],
                                       start=True, stop=True)
                    mm.then_inc(rwT_ready, 1)
                    for slot in range(1, JA + 2):
                        if 2 <= slot < JA:
                            experts_in(slot)
                        if slot <= JR:
                            if slot == 1:
                                pe.wait_ge(rwt_ready, g.count(1, 1))
                            weight(slot - 1)
                        if slot in SLOT_STATES:
                            state(SLOT_STATES[slot])
                        if slot == 1 and prep:
                            prep_transpose()
                        if slot >= 2:
                            experts_out(slot - 2)
                        if slot == 3:
                            for q in range(3):
                                pe.matmul(y_bank[:, :], b2_part[:, q, :], rw_t[:, :], start=False, stop=False)
                        if slot == AT_SILU + 1 and prep:
                            step_sizes(p)
                        if slot == AT_ENDS and prep:
                            bc_proj(p)
                else:
                    if prep:
                        prep_transpose()
                    for slot in sorted(SLOT_STATES):
                        state(SLOT_STATES[slot])
                        if slot == 9:
                            step_sizes(p)
                        if slot == 10:
                            bc_proj(p)
                for n in range(LATE, NS):
                    state(n)
                if mix:
                    if prep:
                        pe.wait_ge(brest_ready, p.count(1, 1))
                        pe.wait_ge(crow_ready, p.count(1, 1))
                    pe.matmul(misc[:, :], ident[:, :], x2[:, g.par, :], start=True, stop=False)
                    pe.wait_ge(v2_ready, g.count(1, 1))
                    add_transposed(v2, ident[:, :], True).then_inc(out_ps, 1)

            run(pe, step)

        @block.vector
        def _(dve):
            dve.memset(vec_rows[:, :], 0.0).then_inc(vz, 1)
            dve.memset(h_t[:, 0, 0:TAPS - 1], 0.0).then_inc(halo_set, 1)
            dve.wait_ge(projT, 1)
            dve.tensor_copy(proj_t[:, :], misc[:, 0:2 * NS + E]).then_inc(proj_ready, 1)
            dve.wait_ge(dtT, 1)
            dve.tensor_copy(dt_t[:, :], p3_bank[0:R, 0:P]).then_inc(dtt_ready, 1)
            dve.wait_ge(condT, 1)
            dve.tensor_copy(cond_t[:, :], in_bank[0][:, 0:NB]).then_inc(condt_ready, 1)
            dve.wait_ge(vecT, 1)
            dve.tensor_copy(vec[:, :], bc_bank[0][:, 0:32]).then_inc(vec_ready, 1)
            dve.wait_ge(proj_ready, 1)
            for a in range(3):
                cp = dve.tensor_copy(bc_w[:, a, :], proj_t[:, 0:2 * NS])
            cp.then_inc(bcw_ready, 1)
            dve.wait_ge(stepw_ps, 1)
            dve.tensor_copy(step_w[:, :], y_bank[:, 0:P]).then_inc(stepw_ready, 1)
            dve.wait_ge(aexp_ready, 1)
            dve.tensor_scalar(a_neg[:, :], a_exp[:, :], -1.0, None, ALU.mult).then_inc(aneg_ready, 1)
            dve.wait_ge(mod_ps, 1)
            dve.tensor_copy(mod[:, :, :].rearrange("p j b -> p (j b)"), p1_bank[:, 0:6 * NB]).then_inc(mod_ready, 1)
            dve.wait_ge(mod_ready, 1)
            for a, j in enumerate((2, 5)):
                dve.tensor_scalar(sign[:, a, :], mod[:, j, :], 0.0, 2.0, ALU.is_ge, ALU.mult).then_inc(mod_a, 1)
                dve.wait_ge(mod_a, 3 * a + 1)
                dve.scalar_tensor_tensor(size[:, a, :], sign[:, a, :], -1.0, mod[:, j, :], ALU.add, ALU.mult)\
                   .then_inc(mod_a, 1)
                dve.wait_ge(mod_a, 3 * a + 2)
                dve.tensor_scalar(size[:, a, :], size[:, a, :], 0.25, None, ALU.max).then_inc(mod_a, 1)
            dve.wait_ge(mod_a, 6)
            dve.tensor_copy(mods[:, :, 0], mod[:, 0, :])
            dve.tensor_scalar(mods[:, :, 1], mod[:, 1, :], 1.0, None, ALU.add)
            dve.scalar_tensor_tensor(mods[:, :, 2], sign[:, 0, :], -1.0, size[:, 0, :], ALU.add, ALU.mult)
            dve.tensor_copy(mods[:, :, 4], mod[:, 3, :])
            dve.tensor_scalar(mods[:, :, 5], mod[:, 4, :], 1.0, None, ALU.add)
            dve.scalar_tensor_tensor(mods[:, :, 6], sign[:, 1, :], -1.0, size[:, 1, :], ALU.add, ALU.mult)\
               .then_inc(mod_b, 1)
            dve.wait_ge(mod_b, 1)
            dve.wait_ge(vec_ready, 1)
            dve.tensor_scalar(mods[:, :, 7], mods[:, :, 6], vec[:, SB2:SB2 + 1], None, ALU.mult)\
               .then_inc(mods_ready, 1)
            dve.tensor_scalar(mods[:, :, 3], mods[:, :, 2], vec[:, DPAR:DPAR + 1], None, ALU.mult).then_inc(mods_b, 1)
            dve.wait_ge(mods_ready, 1)
            dve.wait_ge(mods_b, 1)
            dve.tensor_copy(mod_prep[:, :], mods[:, 0, 0:2]).then_inc(modp_set, 1)
            dve.wait_ge(wm_in, 16 * 13)
            dve.tensor_copy(b2_part[:, 0, :], b2_rows[:, :]).then_inc(b2_a, 1)
            dve.wait_ge(b2_a, 1)
            dve.tensor_tensor(b2_rest[:, :], b2_rows[:, :], b2_part[:, 0, :], ALU.subtract).then_inc(b2_b, 1)
            dve.wait_ge(b2_b, 1)
            dve.tensor_copy(b2_part[:, 1, :], b2_rest[:, :]).then_inc(b2_c, 1)
            dve.wait_ge(b2_c, 1)
            dve.tensor_tensor(b2_part[:, 2, :], b2_rest[:, :], b2_part[:, 1, :], ALU.subtract).then_inc(b2_ready, 1)
            dve.wait_ge(iota_set, 1)

            def moments(k, which, src, s_stats, s_mv, s_ve):
                for s in range(SUB):
                    st = dve.bn_stats(stats[:, which, s, :], src[:, s, :])
                st.then_inc(s_stats, 1)
                dve.wait_ge(s_stats, k.count(1, 1))
                alone(dve)
                for s in range(SUB):
                    ag = dve.bn_aggr(mv[:, which, s, :], stats[:, which, s, :])
                ag.then_inc(s_mv, 1)
                dve.wait_ge(s_mv, k.count(1, 1))
                dve.tensor_scalar(ve[:, which, :], mv[:, which, :, 1], EPS, None, ALU.add).then_inc(s_ve, 1)

            def normalise(k, which, src, s_r, s_nt, s_rstd, s_xn):
                dve.wait_ge(s_r, k.count(1, 1))
                t = nt[:, which, :, :]
                dve.tensor_tensor(t[:, 0, :], r0[:, which, :], r0[:, which, :], ALU.mult).then_inc(s_nt, 1)
                dve.wait_ge(s_nt, k.count(2, 1))
                dve.scalar_tensor_tensor(t[:, 1, :], t[:, 0, :], -0.5, ve[:, which, :], ALU.mult, ALU.mult)\
                   .then_inc(s_nt, 1)
                dve.wait_ge(s_nt, k.count(2, 2))
                dve.scalar_tensor_tensor(rstd[:, which, :], t[:, 1, :], 1.5, r0[:, which, :], ALU.add, ALU.mult)\
                   .then_inc(s_rstd, 1)
                dve.wait_ge(s_rstd, k.count(1, 1))
                for s in range(SUB):
                    ts = dve.tensor_scalar(xn[:, which, s, :], src[:, s, :], mv[:, which, s, 0:1],
                                           rstd[:, which, s:s + 1], ALU.subtract, ALU.mult)
                ts.then_inc(s_xn, 1)

            def prep_moments(k):
                dve.wait_ge(x_in, k.count(16, 16))
                moments(k, 0, x_sb[:, k.par, :, :], st1, mv1, ve1)

            def prep_normalise(k):
                normalise(k, 0, x_sb[:, k.par, :, :], r1, nt1, rstd1, xn1)

            def convolve(k, t):
                h = h_t[:, k.par, :]
                if t == 0:
                    dve.wait_ge(ht_ready, k.count(1, 1))
                    if k.par == 1:
                        dve.tensor_copy(h[:, 0:TAPS - 1], h_t[:, 0, CH:CH + TAPS - 1]).then_inc(halo, 1)
                        dve.wait_ge(halo, (k.off // 2 + 1) if k.i is None else k.i + k.off // 2 + 1)
                    dve.tensor_scalar(cv[:, 0, :], h[:, 0:CH], convw_sb[:, 0:1], None, ALU.mult)\
                       .then_inc(conv_step, 1)
                else:
                    dve.wait_ge(conv_step, k.count(3, t))
                    dve.scalar_tensor_tensor(cv[:, t % 2, :], h[:, t:t + CH], convw_sb[:, t:t + 1],
                                             cv[:, (t - 1) % 2, :], ALU.mult, ALU.add)\
                       .then_inc(conv_step if t < TAPS - 1 else conv_ready, 1)

            def step_miss(k):
                dve.wait_ge(eone_ready, k.count(1, 1))
                dve.scalar_tensor_tensor(miss[:, :], e_one[:, :], 1.0, e_neg[:, :], ALU.subtract, ALU.subtract)\
                   .then_inc(miss_ready, 1)

            def step_base(k):
                dve.wait_ge(miss_ready, k.count(1, 1))
                dve.tensor_tensor(z_pos[:, :], z_pos[:, :], miss[:, :], ALU.subtract).then_inc(base_ready, 1)

            def step_size(k):
                dve.wait_ge(lone_ready, k.count(1, 1))
                dve.scalar_tensor_tensor(l_one[:, :], e_one[:, :], 1.0, l_one[:, :], ALU.is_gt, ALU.mult)\
                   .then_inc(lzero_ready, 1)
                dve.wait_ge(base_ready, k.count(1, 1))
                if k.i is not None or k.off:
                    dve.wait_ge(decay_ready, k.count(NS, 0))
                dve.wait_ge(lzero_ready, k.count(1, 1))
                dve.tensor_tensor(dt_sb[:, :], l_one[:, :], z_pos[:, :], ALU.add).then_inc(dt_ready, 1)

            def scan_input(k):
                dve.wait_ge(dt_ready, k.count(1, 1))
                dve.tensor_tensor(u_sb[:, k.par, :], dt_sb[:, :], xc[:, k.par, :], ALU.mult).then_inc(u_ready, 1)

            def b_remainder(k):
                dve.wait_ge(bhi_ready, k.count(1, 1))
                dve.wait_ge(crow_ready, k.count(1, 1))
                dve.tensor_tensor(b_rest[:, :], misc[0:96, :], b_split[:, k.par, :], ALU.subtract)\
                   .then_inc(brest_ready, 1)

            def b_low(k):
                dve.wait_ge(bmid_ready, k.count(2, 2))
                low = b_split[64:96, k.par, :]
                dve.tensor_tensor(low, b_rest[64:96, :], low, ALU.subtract).then_inc(b_ready, 1)

            prep_moments(Chunk(0))
            prep_normalise(Chunk(0))
            for t in range(TAPS):
                convolve(Chunk(0), t)
            b_remainder(Chunk(0))
            b_low(Chunk(0))
            step_miss(Chunk(0))
            step_base(Chunk(0))
            step_size(Chunk(0))
            scan_input(Chunk(0))

            def step(number, c, scan, mix, prep):
                g, p = c.plus(-1), c.plus(1)
                order = ring_order(scan, mix)
                start = ring_start(number)

                def spread(kind, n):
                    return bc_bank[(start + order.index((kind, n))) % 2]

                def scan_state(n):
                    dve.wait_ge(ub_done, c.count(NS, n + 1))
                    dve.wait_ge(decay_ready, c.count(NS, n + 1))
                    if n >= HRING or number:
                        dve.wait_ge(cmul, c.count(NS, n - HRING + 1))
                    first = 0.0
                    if c.par == 1:
                        dve.wait_ge(carry_done, (c.off // 2 * NS + n + 1) if c.i is None
                                    else c.i * NS + (c.off // 2 * NS + n + 1))
                        first = carry[:, n:n + 1]
                    dve.tensor_tensor_scan(h_s[:, n % HRING, :], decay[:, n, :], in_bank[n % 2][:, :],
                                           first, ALU.mult, ALU.add).then_inc(scan_done, 1)

                def state_input(n):
                    if not scan:
                        return
                    if n == 0:
                        dve.wait_ge(u_ready, c.count(1, 1))
                    dve.wait_ge(bb_ready, c.count(NS, n + 1))
                    if n >= 2 or number:
                        dve.wait_ge(scan_done, c.count(NS, n - 1))
                    dve.tensor_tensor(in_bank[n % 2][:, :], u_sb[:, c.par, :], spread("N", n)[:, :], ALU.mult)\
                       .then_inc(ub_done, 1)

                def hidden(j):
                    m = width(j)
                    dve.wait_ge(u3_done, g.count(JA, j + 1))
                    dve.wait_ge(p1_ready, g.count(JA, j + 1))
                    if j >= 2:
                        dve.wait_ge(s_done, g.count(JA, j - 1))
                    dve.scalar_tensor_tensor(z_sb[0:m, j % 2, :], p1_bank[0:m, :],
                                             vec[0:m, B1 + j:B1 + j + 1], u3[0:m, j % 2, :],
                                             ALU.add, ALU.mult).then_inc(z_done, 1)

                def weigh(j):
                    dve.wait_ge(s_done, g.count(JA, j + 1))
                    dve.wait_ge(rwb_ready, g.count(JR, j + 1))
                    if j >= HP:
                        dve.wait_ge(w2_done, g.count(JA, j - HP + 1))
                    dve.tensor_tensor(hg[:, j % HP, :], s_sb[:, j % 2, :], spread("R", j)[:, :],
                                      ALU.mult).then_inc(hg_done, 1)

                if number % 2 == 1 and mix:
                    b = g.off // 2 if g.i is None else g.i + g.off // 2
                    dve.tensor_copy(mod_gate[:, :], mods[:, b, 2:4]).then_inc(modg_set, 1)
                    dve.wait_ge(modg_set, (g.off // 2 + 1) if g.i is None else g.i + g.off // 2 + 1)
                    dve.tensor_scalar(gate_diag[:, 0, :], ident[:, :], mod_gate[:, 0:1], None, ALU.mult)
                    dve.tensor_scalar(gate_diag[:, 1, :], ident[:, :], mod_gate[:, 1:2], None, ALU.mult)\
                       .then_inc(diag_set, 1)
                    if prep:
                        b = p.off // 2 if p.i is None else p.i + p.off // 2
                        dve.tensor_copy(mod_prep[:, :], mods[:, b, 0:2]).then_inc(modp_set, 1)
                state_input(0)
                state_input(1)
                if scan:
                    scan_state(0)
                state_input(2)
                if scan:
                    scan_state(1)
                if mix:
                    dve.wait_ge(x2_ready, g.count(1, 1))
                    moments(g, 1, misc_t, st2, mv2, ve2)
                    if number % 2 == 1:
                        b = g.off // 2 if g.i is None else g.i + g.off // 2
                        dve.tensor_copy(mod_mix[:, :], mods[:, b, 4:8]).then_inc(modm_set, 1)
                state_input(3)
                if prep:
                    prep_moments(p)
                if scan:
                    scan_state(2)
                if mix:
                    dve.wait_ge(x2_done, g.count(1, 1))
                    normalise(g, 1, x2[:, g.par, :].rearrange("p (s d) -> p s d", s=SUB), r2, nt2, rstd2, xn2)
                if scan:
                    scan_state(3)
                for n in range(4, EARLY):
                    state_input(n)
                if mix:
                    dve.wait_ge(h2_ready, g.count(1, 1))
                    dve.tensor_scalar(h2_m.bitcast(U32), h2_t[:, :].bitcast(U32), HIGH_BITS, None,
                                      ALU.bitwise_and).then_inc(hh_ready, 1)
                    logits = misc[:, 0:SUB * E].rearrange("p (s e) -> p s e", s=SUB)
                    dve.wait_ge(lg_ready, g.count(1, 1))
                    dve.tensor_reduce(nmax[:, :], logits, AX.X, ALU.max, negate=True).then_inc(nmax_ready, 1)
                    dve.wait_ge(hh_ready, g.count(1, 1))
                    dve.tensor_copy(h2_hi[:, :], h2_m)
                    dve.tensor_tensor(h2_lo[:, :], h2_t[:, :], h2_m, ALU.subtract)\
                       .then_inc(h2s_ready, 1)
                    dve.wait_ge(nmax_ready, g.count(1, 1))
                    dve.tensor_tensor(ls[:, :, :], logits, nmax[:, :].unsqueeze(2).broadcast_to([P, SUB, E]),
                                      ALU.add).then_inc(ls_ready, 1)
                if scan:
                    for n in range(4, EARLY):
                        scan_state(n)
                if prep:
                    prep_normalise(p)
                if mix:
                    dve.wait_ge(ge_ready, g.count(1, 1))
                    dve.tensor_reduce(gsum[:, :], ge[:, :, :], AX.X, ALU.add).then_inc(gsum_ready, 1)
                    dve.wait_ge(gsum_ready, g.count(1, 1))
                    dve.reciprocal(grec[:, :], gsum[:, :]).then_inc(grec_ready, 1)
                    dve.wait_ge(grec_ready, g.count(1, 1))
                    dve.tensor_tensor(score[:, :, :], ge[:, :, :], grec[:, :].unsqueeze(2).broadcast_to([P, SUB, E]),
                                      ALU.mult).then_inc(score_ready, 1)
                    dve.wait_ge(score_ready, g.count(1, 1))
                    dve.tensor_tensor(biased[:, :, :], score[:, :, :],
                                      gateb_sb[:, :].unsqueeze(1).broadcast_to([P, SUB, E]), ALU.add)\
                       .then_inc(biased_ready, 1)
                    hidden(0)
                    dve.wait_ge(biased_ready, g.count(1, 1))
                    alone(dve)
                    for s in range(SUB):
                        mx = dve.max(top[:, s, :], biased[:, s, :])
                    mx.then_inc(top_ready, 1)
                    dve.wait_ge(top_ready, g.count(1, 1))
                    alone(dve)
                    for s in range(SUB):
                        mx = dve.max_index(topi[:, s, :], top[:, s, :], biased[:, s, :])
                    mx.then_inc(topi_ready, 1)
                    dve.wait_ge(topi_ready, g.count(1, 1))
                    dve.tensor_copy(topf[:, :, :], topi[:, :, 0:2]).then_inc(topf_ready, 1)
                    dve.wait_ge(topf_ready, g.count(1, 1))
                    for a in range(2):
                        eq = dve.tensor_tensor(hot[:, a, :, :], iota_f[:, :].unsqueeze(1).broadcast_to([P, SUB, E]),
                                               topf[:, :, a:a + 1].broadcast_to([P, SUB, E]), ALU.is_equal)
                    eq.then_inc(hot_ready, 1)
                    dve.wait_ge(hot_ready, g.count(1, 1))
                    dve.tensor_tensor(hot[:, 0, :, :], hot[:, 0, :, :], hot[:, 1, :, :], ALU.add)\
                       .then_inc(hots_ready, 1)
                    dve.wait_ge(hots_ready, g.count(1, 1))
                    dve.tensor_tensor(rw[:, :, :], score[:, :, :], hot[:, 0, :, :], ALU.mult).then_inc(rw_ready, 1)
                    dve.wait_ge(rw_ready, g.count(1, 1))
                    dve.tensor_copy(rw_part[:, :, 0, :], rw[:, :, :]).then_inc(rwh_ready, 1)
                    dve.wait_ge(rwh_ready, g.count(1, 1))
                    dve.tensor_tensor(rw_rest[:, :, :], rw[:, :, :], rw_part[:, :, 0, :], ALU.subtract)\
                       .then_inc(rwr_ready, 1)
                    dve.wait_ge(rwr_ready, g.count(1, 1))
                    dve.tensor_copy(rw_part[:, :, 1, :], rw_rest[:, :, :]).then_inc(rwm_ready, 1)
                    dve.wait_ge(rwm_ready, g.count(1, 1))
                    dve.tensor_tensor(rw_part[:, :, 2, :], rw_rest[:, :, :], rw_part[:, :, 1, :], ALU.subtract)\
                       .then_inc(r3_ready, 1)
                if number == 0:
                    dve.wait_ge(w_in, 16 * 4)
                    for part, whole in ((w1_m, w1_all), (w3_m, w3_all)):
                        dve.tensor_scalar(part.bitcast(U32), whole.bitcast(U32), HIGH_BITS, None,
                                          ALU.bitwise_and).then_inc(whi_ready, 1)
                    for q, (hi, lo, part, whole) in enumerate(((w1_hi, w1_lo, w1_m, w1_all),
                                                               (w3_hi, w3_lo, w3_m, w3_all))):
                        dve.wait_ge(whi_ready, q + 1)
                        dve.tensor_copy(hi[:, :], part)
                        dve.tensor_tensor(lo[:, :], whole, part, ALU.subtract).then_inc(wsplit_ready, 1)
                pending = None
                for slot in range(1, JA + 1):
                    if mix and slot < JA:
                        hidden(slot)
                    if pending is not None:
                        scan_state(pending)
                        pending = None
                    if mix and slot <= JR:
                        weigh(slot - 1)
                    if scan and slot in SLOT_STATES:
                        pending = SLOT_STATES[slot]
                        state_input(pending)
                    if prep:
                        if AT_CONV <= slot < AT_CONV + TAPS:
                            convolve(p, slot - AT_CONV)
                        if slot == AT_SOFT:
                            b_remainder(p)
                            step_miss(p)
                            step_base(p)
                        if slot == AT_SOFT + 1:
                            step_size(p)
                            scan_input(p)
                        if slot == AT_SOFT + 2:
                            b_low(p)
                if scan:
                    for n in range(LATE, NS):
                        state_input(n)
                        scan_state(n - 1)
                    scan_state(NS - 1)

            run(dve, step)


_INS = ['L0_attn_x', 'L0_attn_conv_w', 'L0_attn_conv_b', 'L0_attn_x_proj_dt_w', 'L0_attn_dt_proj_w',
        'L0_attn_dt_proj_b', 'L0_attn_B_proj_w', 'L0_attn_C_proj_w', 'L0_attn_A_log', 'L0_attn_D_param',
        'L0_ffn_gate_w', 'L0_ffn_gate_b', 'L0_ffn_w1', 'L0_ffn_b1', 'L0_ffn_w3', 'L0_ffn_b3', 'L0_ffn_w2',
        'L0_ffn_b2', 'L0_ffn_sw1', 'L0_ffn_sb1', 'L0_ffn_sw3', 'L0_ffn_sb3', 'L0_ffn_sw2', 'L0_ffn_sb2',
        'L0_c', 'L0_wmod']
_OUTS = [((4, 1024, 128), 'float32')]


def kernel(**inputs):
    import numpy as _np
    import concourse.bacc as _bacc
    from concourse import mybir as _mybir
    from concourse.bass_utils import run_bass_kernel_spmd as _run

    nc = _bacc.Bacc("TRN2", target_bir_lowering=False, num_devices=1)
    arrays, args = {}, []
    for name in _INS:
        a = _np.ascontiguousarray(inputs[name])
        arrays[f"in_{name}_dram"] = a
        args.append(nc.dram_tensor(f"in_{name}_dram", a.shape, _mybir.dt.from_np(a.dtype), kind="ExternalInput").ap())
    for i, (shape, dtype) in enumerate(_OUTS):
        dt = _mybir.dt.from_np(_np.dtype(dtype))
        args.append(nc.dram_tensor(f"out_{i}_dram", shape, dt, kind="ExternalOutput").ap())
    adaln_kernel(nc, *args)
    r = _run(nc, [arrays], core_ids=[0])
    got = tuple(r.results[0][f"out_{i}_dram"] for i in range(len(_OUTS)))
    return got[0]
```

```python
from contextlib import ExitStack

import concourse.bass as bass
from concourse import mybir

ALU = mybir.AluOpType
ACT = mybir.ActivationFunctionType
AX = mybir.AxisListType
F32 = mybir.dt.float32
BF16 = mybir.dt.bfloat16
U32 = mybir.dt.uint32
F32R = mybir.dt.float32r
HIGH_BITS = 0xFFFFF000

P = 128
CH = 512
SUB = CH // P
NB = 4
L = 1024
NCH = NB * L // CH
NS = 16
TAPS = 4
R = 64
E = 8
H = 176
HR = E * H
HA = HR + H
JR = HR // P
JA = -(-HA // P)
LAST = HA - (JA - 1) * P
EPS = 1e-5
HRING = 4
HP = 3
assert HR % P == 0


def width(j):
    return P if j < JA - 1 else LAST


class Chunk:

    def __init__(self, off, i=None, mult=0):
        self.off, self.i, self.mult = off, i, mult
        self.par = off % 2

    def plus(self, d):
        return Chunk(self.off + d, self.i, self.mult)

    def count(self, per, extra):
        v = self.off * per + extra
        return v if self.i is None else self.i * (self.mult * per) + v


EARLY = 8
SLOT_STATES = {1: 8, 3: 9, 5: 10, 7: 11, 9: 12, 10: 13, 11: 14, 12: 15}
assert EARLY + len(SLOT_STATES) == NS
DECAYS_0, DECAYS_1, DECAYS_2 = 4, 11, 15
AT_HT, AT_CONV, AT_SILU, AT_ENDS, AT_SPLIT, AT_SOFT, AT_MID = 3, 3, 7, 8, 9, 10, 11
POOL_BASE = 12
ROUTER_STAGES = 14
STEPS = NCH + 2


def ring_order(number):
    scan, experts = number < NCH, number >= 2
    out = [("N", n) for n in range(EARLY)] if scan else []
    for slot in range(1, JA + 1):
        if experts and slot <= JR:
            out.append(("R", slot - 1))
        if scan and slot in SLOT_STATES:
            out.append(("N", SLOT_STATES[slot]))
    return out


def ring_start(number):
    return sum(len(ring_order(n)) for n in range(number))


def adaln_kernel(nc, x, conv_w, conv_b, xdt_w, dt_w, dt_b, b_w, c_w, a_log, d_par, gate_w, gate_b,
                 w1, b1, w3, b3, w2, b2, sw1, sb1, sw3, sb3, sw2, sb2, cond, wmod, out):
    x_tok = x.rearrange("b (k s p) d -> (b k) p s d", p=P, s=SUB)
    out_tok = out.rearrange("b (k s p) d -> (b k) p s d", p=P, s=SUB)
    c_dram = nc.dram_tensor("c_scratch", (2, NS, CH), F32).ap()

    with ExitStack() as ctx:
        def sb(name, shape, dt=F32):
            return ctx.enter_context(nc.sbuf_tensor(name, shape, dt))

        def bank(name, dt=F32):
            return ctx.enter_context(nc.psum_tensor(name, [P, CH], dt))

        def sem(name):
            return ctx.enter_context(nc.semaphore(name))

        w1_hi = sb("w1_hi", [P, HA], F32R)
        w1_lo = sb("w1_lo", [P, HA], F32R)
        w3_hi = sb("w3_hi", [P, HA], F32R)
        w3_lo = sb("w3_lo", [P, HA], F32R)
        w2_sb = sb("w2_sb", [P, JA, P])
        vec_rows = sb("vec_rows", [32, P])
        vec = sb("vec", [P, 32])
        B1, B3, CONVB, DPAR, DTB, SB2 = 0, JA, 2 * JA, 2 * JA + 1, 2 * JA + 2, 2 * JA + 3
        proj_rows = sb("proj_rows", [2 * NS + E, P])
        proj_t = sb("proj_t", [P, 2 * NS + E])
        bc_w = sb("bc_w", [P, 3, 2 * NS])
        cond_rows = sb("cond_rows", [NB, P])
        cond_act = sb("cond_act", [NB, P])
        cond_t = sb("cond_t", [P, NB])
        xdt_sb = sb("xdt_sb", [R, P])
        dt_rows = sb("dt_rows", [P, R])
        dt_t = sb("dt_t", [R, P])
        step_w = sb("step_w", [P, P])
        convw_sb = sb("convw_sb", [P, TAPS])
        alog_sb = sb("alog_sb", [P, NS])
        a_exp = sb("a_exp", [P, NS])
        a_neg = sb("a_neg", [P, NS])
        gateb_sb = sb("gateb_sb", [P, E])
        b2_rows = sb("b2_rows", [3 * E, P])
        b2_rest = sb("b2_rest", [3 * E, P])
        b2_part = sb("b2_part", [3 * E, 3, P], BF16)
        mod = sb("mod", [P, 6, NB])
        sign = sb("sign", [P, 2, NB])
        size = sb("size", [P, 2, NB])
        mods = sb("mods", [P, NB, 8])
        mod_prep = sb("mod_prep", [P, 2])
        mod_head = sb("mod_head", [P, 2])
        mod_tail = sb("mod_tail", [P, 2])
        mod_gate = sb("mod_gate", [P, 2])
        gate_diag = sb("gate_diag", [P, 2, P])
        probe = sb("probe", [P, 1])
        ident = sb("ident", [P, P])
        ident_b = sb("ident_b", [P, P], BF16)
        sel_state = sb("sel_state", [3 * 32, NS, P], BF16)
        sel_expert = sb("sel_expert", [3 * E, JR, P], BF16)
        iota_f = sb("iota_f", [P, E])

        x_sb = sb("x_sb", [P, 2, SUB, P])
        stats = sb("stats", [P, 2, SUB, 6])
        mv = sb("mv", [P, 2, SUB, 2])
        ve = sb("ve", [P, 2, SUB])
        half = sb("half", [P, 2, SUB])
        r0 = sb("r0", [P, 2, SUB])
        nt = sb("nt", [P, 2, 2, SUB])
        rstd = sb("rstd", [P, 2, SUB])
        shift = sb("shift", [P, 2, SUB])
        xn = sb("xn", [P, 2, SUB, P])
        h_t = sb("h_t", [P, 2, TAPS - 1 + CH])
        cv = sb("cv", [P, 2, CH])
        e_one, miss = cv[:, 0, :], cv[:, 1, :]
        xc = sb("xc", [P, 2, CH])
        z_abs = sb("z_abs", [P, CH])
        z_pos = sb("z_pos", [P, CH])
        e_neg = z_abs
        l_one = sb("l_one", [P, CH])
        dt_sb = sb("dt_sb", [P, CH])
        u_sb = sb("u_sb", [P, 2, CH])
        b_split = sb("b_split", [96, 2, CH], BF16)
        b_rest = sb("b_rest", [96, CH])
        c_rows = sb("c_rows", [32, CH])
        c_all = sb("c_all", [P, NS, CH])
        decay = sb("decay", [P, NS, CH])
        wmod_sb = decay[:, 14:16, :].rearrange("p n t -> p (n t)")[:, 0:6 * P]
        sel_part = decay[0:3 * E, 8:13, :].rearrange("p n t -> p (n t)").bitcast(BF16)[:, 0:3 * JR * P]\
            .rearrange("p (g f) -> p g f", g=3)
        h_s = sb("h_s", [P, HRING, CH])
        hc = sb("hc", [P, 2, CH])
        carry = sb("carry", [P, NS])
        acc = sb("acc", [P, 2, CH])
        mix_work = sb("mix_work", [P, 11 + HP, CH])
        x2, o_sb = mix_work[:, 0:2, :], mix_work[:, 2:4, :]
        v2 = mix_work[:, 4, :]
        u3, z_sb, s_sb = mix_work[:, 5:7, :], mix_work[:, 7:9, :], mix_work[:, 9:11, :]
        hg = mix_work[:, 11:, :]
        h2_m = v2
        w_flat = mix_work[:, :, :].rearrange("p n t -> p (n t)")
        w1_all, w3_all = w_flat[:, 0:HA], w_flat[:, HA:2 * HA]
        w1_m, w3_m = w_flat[:, 2 * HA:3 * HA], w_flat[:, 3 * HA:4 * HA]
        assert 4 * HA <= (11 + HP) * CH
        h2_t = sb("h2_t", [P, CH])
        h2_hi = sb("h2_hi", [P, 2, CH], F32R)
        h2_lo = sb("h2_lo", [P, 2, CH], F32R)
        nmax = sb("nmax", [P, SUB])
        ls = sb("ls", [P, SUB, E])
        ge = sb("ge", [P, SUB, E])
        gsum = sb("gsum", [P, SUB])
        grec = sb("grec", [P, SUB])
        score = sb("score", [P, SUB, E])
        biased = sb("biased", [P, SUB, E])
        top = sb("top", [P, SUB, 8])
        topi = sb("topi", [P, SUB, 8], U32)
        topf = sb("topf", [P, SUB, 2])
        hot = sb("hot", [P, 2, SUB, E])
        rw = sb("rw", [P, SUB, E])
        rw_rest = sb("rw_rest", [P, SUB, E])
        rw_part = sb("rw_part", [P, SUB, 3, E], BF16)
        rw_t = sb("rw_t", [3 * E, 2, CH], BF16)

        bc_bank = [bank("bc0"), bank("bc1")]
        in_bank = [bank("in0"), bank("in1")]
        p3_bank = bank("p3_bank")
        p1_bank = bank("p1_bank")
        y_bank = bank("y_bank")
        misc = bank("misc")
        misc_t = misc[:, :].rearrange("p (s d) -> p s d", s=SUB)

        names = """w_in wr_in w2_in wm_in vz x_in ones_set id_set idb_set selz sel_s selp sel_e iota_set halo_set
        vecT vec_ready projT proj_ready bcw_ready cond_ready condT condt_ready dtT dtt_ready stepw_ps stepw_ready
        mod_ps mod_ready mod_a mod_b mods_ready aexp_ready aneg_ready b2_a b2_b b2_c b2_ready modp_set modm_set modt_set modg_set
        st_done st2_done mv_done ve_done r_done nt_step rstd_done xn1 xnT1 tap0_ready ht_ready halo conv_step conv_ready xc_ready zdt_ready zdt_abs zdt_used
        eneg_ready eone_ready lone_ready lzero_ready miss_ready dt_ready u_ready bcp_ready bhi_ready crow_ready
        brest_ready bmid_ready b_ready c_dram_in decay_ready
        bb_ready ub_done scan_done carry_done cmul acc_step acc_ready
        x_used x2_ready x2_done diag_set mods_b xn2 xnT2 h2_ready hh_ready h2s_ready whi_ready wsplit_ready half_set base_ready lg_ready nmax_ready ls_ready
        ge_ready gsum_ready grec_ready score_ready biased_ready top_ready topi_ready topf_ready hot_ready hots_ready
        rw_ready rwh_ready rwr_ready rwm_ready r3_ready rwT_ready rwt_ready
        p3_ready u3_done p1_ready z_done s_done rwb_ready hg_done w2_done v2_ready out_ps out_ready
        st_out"""
        S = {n: sem(n) for n in names.split()}
        (w_in, wr_in, w2_in, wm_in, vz, x_in, ones_set, id_set, idb_set, selz, sel_s, selp, sel_e, iota_set,
         halo_set, vecT, vec_ready, projT, proj_ready, bcw_ready, cond_ready, condT, condt_ready, dtT, dtt_ready,
         stepw_ps, stepw_ready, mod_ps, mod_ready, mod_a, mod_b, mods_ready, aexp_ready, aneg_ready, b2_a, b2_b,
         b2_c, b2_ready, modp_set, modm_set, modt_set, modg_set, st_done, st2_done, mv_done, ve_done, r_done, nt_step, rstd_done, xn1, xnT1, tap0_ready, ht_ready, halo, conv_step,
         conv_ready, xc_ready, zdt_ready, zdt_abs, zdt_used, eneg_ready, eone_ready, lone_ready, lzero_ready, miss_ready,
         dt_ready, u_ready, bcp_ready, bhi_ready, crow_ready, brest_ready, bmid_ready, b_ready,
         c_dram_in, decay_ready, bb_ready, ub_done, scan_done, carry_done, cmul, acc_step, acc_ready, 
         x_used, x2_ready, x2_done, diag_set, mods_b, xn2, xnT2, h2_ready, hh_ready, h2s_ready, whi_ready, wsplit_ready, half_set, base_ready, lg_ready, nmax_ready,
         ls_ready, ge_ready, gsum_ready, grec_ready, score_ready, biased_ready, top_ready, topi_ready, topf_ready,
         hot_ready, hots_ready, rw_ready, rwh_ready, rwr_ready, rwm_ready, r3_ready, rwT_ready, rwt_ready,
         p3_ready, u3_done, p1_ready, z_done, s_done, rwb_ready, hg_done, w2_done, v2_ready, out_ps,
         out_ready, st_out) = S.values()
        c_in = [sem(f"c_in{g}") for g in range(4)]

        block = ctx.enter_context(nc.Block())

        def alone(eng):
            eng.nop(nofuse=True)

        def run(eng, step):
            step(0, Chunk(0))
            step(1, Chunk(1))
            with eng.Fori(0, (NCH - 4) // 2) as i:
                step(2, Chunk(2, i, 2))
                step(3, Chunk(3, i, 2))
            for number in range(NCH - 2, STEPS):
                step(number, Chunk(number))

        def stages(number):
            return number < NCH - 1, number < NCH, 1 <= number <= NCH, number >= 2

        @block.sync
        def _(sp):
            def rows(dst, src, s):
                sp.dma_start(dst, src).then_inc(s, 16)

            def one(v):
                return v.rearrange("(a n) -> a n", a=1)

            rows(x_sb[:, 0, :, :], x_tok[0], x_in)
            sp.wait_ge(vz, 1)
            rows(vec_rows[B1:B1 + JR, :], b1.rearrange("e h -> (e h)").rearrange("(k p) -> k p", p=P), wr_in)
            rows(vec_rows[B1 + JR:B1 + JR + 1, :], one(sb1)[:, 0:P], wr_in)
            rows(vec_rows[B1 + JR + 1:B1 + JA, 0:LAST], one(sb1)[:, P:H], wr_in)
            rows(vec_rows[B3:B3 + JR, :], b3.rearrange("e h -> (e h)").rearrange("(k p) -> k p", p=P), wr_in)
            rows(vec_rows[B3 + JR:B3 + JR + 1, :], one(sb3)[:, 0:P], wr_in)
            rows(vec_rows[B3 + JR + 1:B3 + JA, 0:LAST], one(sb3)[:, P:H], wr_in)
            rows(vec_rows[CONVB:CONVB + 1, :], one(conv_b), wr_in)
            rows(vec_rows[DPAR:DPAR + 1, :], one(d_par), wr_in)
            rows(vec_rows[DTB:DTB + 1, :], one(dt_b), wr_in)
            rows(vec_rows[SB2:SB2 + 1, :], one(sb2), wr_in)
            rows(w1_all[:, 0:HR].rearrange("p (e h) -> p e h", e=E), w1.rearrange("e d h -> d e h"), w_in)
            rows(w1_all[:, HR:HA], sw1, w_in)
            rows(w3_all[:, 0:HR].rearrange("p (e h) -> p e h", e=E), w3.rearrange("e d h -> d e h"), w_in)
            rows(w3_all[:, HR:HA], sw3, w_in)
            rows(w2_sb[:, 0:JR, :], w2.rearrange("e h d -> (e h) d").rearrange("(k p) d -> p k d", p=P), w2_in)
            rows(w2_sb[:, JR, :], sw2[0:P, :], w2_in)
            rows(w2_sb[0:LAST, JR + 1, :], sw2[P:H, :], w2_in)

            def load_x(k):
                if k.i is not None or k.off >= 2:
                    sp.wait_ge(x_used, k.plus(-2).count(1, 1))
                    alone(sp)
                num = k.off if k.i is None else k.i * k.mult + k.off
                sp.dma_start(x_sb[:, k.par, :, :], x_tok[num]).then_inc(x_in, 16)

            def save_c(k):
                sp.wait_ge(crow_ready, k.count(1, 1))
                sp.dma_start(c_dram[k.par], c_rows[NS:2 * NS, :]).then_inc(c_dram_in, 16)
                sp.wait_ge(c_dram_in, k.count(16, 16))
                alone(sp)

            def spread_c(k, g):
                if k.i is not None or k.off:
                    sp.wait_ge(cmul, k.count(NS, 4 * g + 4 - NS))
                src = c_dram[k.par, 4 * g:4 * g + 4, :].rearrange("(a n) t -> a n t", a=1)
                sp.dma_start(c_all[:, 4 * g:4 * g + 4, :], src.broadcast_to([P, 4, CH])).then_inc(c_in[g], 16)

            def store(k):
                sp.wait_ge(out_ready, k.count(1, 2))
                alone(sp)
                num = k.off if k.i is None else k.i * k.mult + k.off
                sp.dma_start(out_tok[num], o_sb[:, k.par, :].rearrange("p (s d) -> p s d", s=SUB))\
                  .then_inc(st_out, 16)
                sp.wait_ge(st_out, k.count(16, 16))
                alone(sp)

            save_c(Chunk(0))
            for g in range(4):
                spread_c(Chunk(0), g)

            def step(number, c):
                prep, scan, head, experts = stages(number)
                if prep:
                    load_x(c.plus(1))
                    save_c(c.plus(1))
                    for g in range(4):
                        spread_c(c.plus(1), g)
                if experts:
                    store(c.plus(-2))

            run(sp, step)

        @block.gpsimd
        def _(pool):
            pool.memset(half[:, :, :], -0.5).then_inc(half_set, 1)
            pool.memset(ident[:, :], 0.0).then_inc(ones_set, 1)
            pool.memset(ident_b[:, :], 0.0).then_inc(ones_set, 1)
            pool.memset(sel_state[:, :, :], 0.0).then_inc(ones_set, 1)
            pool.memset(sel_part[:, :, :], 1.0).then_inc(ones_set, 1)
            pool.wait_ge(ones_set, 4)
            pool.affine_select(out=ident[:, :], in_=ident[:, :], compare_op=ALU.not_equal, fill=1.0, base=0,
                               pattern=[[-1, P]], channel_multiplier=1).then_inc(id_set, 1)
            pool.affine_select(out=ident_b[:, :], in_=ident_b[:, :], compare_op=ALU.not_equal, fill=1.0, base=0,
                               pattern=[[-1, P]], channel_multiplier=1).then_inc(idb_set, 1)
            def rsqrt_start(steps, lo, hi):
                pool.wait_ge(ve_done, steps)
                pool.tensor_tensor(r0[:, lo:hi, :], ve[:, lo:hi, :], half[:, lo:hi, :], ALU.pow).then_inc(r_done, 1)

            pool.wait_ge(half_set, 1)
            rsqrt_start(1, 0, 1)
            for g in range(3):
                pool.affine_select(out=sel_state[:, :, :], in_=sel_state[:, :, :], compare_op=ALU.not_equal,
                                   fill=1.0, base=-32 * g, pattern=[[-1, NS], [0, P]], channel_multiplier=1)\
                    .then_inc(sel_s, 1)
                pool.wait_ge(sel_s, g + 1)
            for g in range(3):
                part = sel_part[:, g, :]
                pool.affine_select(out=part, in_=part, compare_op=ALU.is_ge, fill=0.0, base=H * E * g,
                                   pattern=[[1, JR * P]], channel_multiplier=-H).then_inc(selp, 1)
                pool.wait_ge(selp, 2 * g + 1)
                pool.affine_select(out=part, in_=part, compare_op=ALU.is_ge, fill=0.0, base=H - 1 - H * E * g,
                                   pattern=[[-1, JR * P]], channel_multiplier=H).then_inc(selp, 1)
                pool.wait_ge(selp, 2 * g + 2)
            flat = sel_expert[:, :, :].rearrange("r j m -> r (j m)")
            pool.tensor_tensor(flat, sel_part[:, 0, :], sel_part[:, 1, :], ALU.add).then_inc(sel_e, 1)
            pool.wait_ge(sel_e, 1)
            pool.tensor_tensor(flat, flat, sel_part[:, 2, :], ALU.add).then_inc(sel_e, 1)
            pool.iota(iota_f[:, :], [[1, E]], base=0, channel_multiplier=0,
                      allow_small_or_imprecise_dtypes=True).then_inc(iota_set, 1)

            def state(k, n):
                if n == 1 and (k.i is not None or k.off):
                    pool.wait_ge(acc_step, k.count(NS - 1, 0))
                pool.wait_ge(scan_done, k.count(NS, n + 1))
                if n % 4 == 0:
                    pool.wait_ge(c_in[n // 4], k.count(16, 16))
                h = h_s[:, n % HRING, :]
                if k.par == 0:
                    alone(pool)
                    pool.tensor_copy(carry[:, n:n + 1], h[:, CH - 1:CH]).then_inc(carry_done, 1)
                dst = acc[:, k.par, :] if n == 0 else hc[:, n % 2, :]
                if n >= 3:
                    pool.wait_ge(acc_step, k.count(NS - 1, n - 2))
                pool.tensor_tensor(dst, h, c_all[:, n, :], ALU.mult).then_inc(cmul, 1)

            def add(k, n):
                pool.wait_ge(cmul, k.count(NS, n + 1))
                if n >= 2:
                    pool.wait_ge(acc_step, k.count(NS - 1, n - 1))
                a = acc[:, k.par, :]
                pool.tensor_tensor(a, a, hc[:, n % 2, :], ALU.add).then_inc(acc_step, 1)

            def step_base(k):
                pool.wait_ge(miss_ready, k.count(1, 1))
                pool.tensor_tensor(z_pos[:, :], z_pos[:, :], miss, ALU.subtract).then_inc(base_ready, 1)

            step_base(Chunk(0))

            def step(number, c):
                prep, scan, head, experts = stages(number)
                for n in range(NS if prep or head else 0):
                    if scan:
                        state(c, n)
                        if n >= 2:
                            add(c, n - 1)
                    if n == 2:
                        rsqrt_start(c.count(1, 2), 0 if prep else 1, 2 if head else 1)
                    if n == POOL_BASE and prep:
                        step_base(c.plus(1))
                if scan:
                    add(c, NS - 1)

            run(pool, step)

        @block.scalar
        def _(act):
            act.dma_start(proj_rows[0:NS, :], b_w).then_inc(wm_in, 16)
            act.dma_start(proj_rows[NS:2 * NS, :], c_w).then_inc(wm_in, 16)
            act.dma_start(proj_rows[2 * NS:2 * NS + E, :], gate_w).then_inc(wm_in, 16)
            act.dma_start(cond_rows[:, :], cond).then_inc(wm_in, 16)
            act.dma_start(xdt_sb[:, :], xdt_w).then_inc(wm_in, 16)
            act.dma_start(dt_rows[:, :], dt_w).then_inc(wm_in, 16)
            act.dma_start(convw_sb[:, :], conv_w.rearrange("d a t -> d (a t)")).then_inc(wm_in, 16)
            act.dma_start(alog_sb[:, :], a_log).then_inc(wm_in, 16)
            act.dma_start(gateb_sb[:, :], gate_b.rearrange("(a n) -> a n", a=1).broadcast_to([P, E]))\
               .then_inc(wm_in, 16)
            act.dma_start(wmod_sb[:, :], wmod).then_inc(wm_in, 16)
            for g in range(3):
                act.dma_start(b2_rows[E * g:E * g + E, :], b2).then_inc(wm_in, 16)
            def normalise(which, src, steps, done):
                act.wait_ge(rstd_done, steps)
                for s in range(SUB):
                    ac = act.activation(xn[:, which, s, :], src[:, s, :], ACT.Identity,
                                        bias=shift[:, which, s:s + 1], scale=rstd[:, which, s:s + 1])
                ac.then_inc(done, 1)

            normalise(0, x_sb[:, 0, :, :], 2, xn1)
            act.wait_ge(wm_in, 16 * 13)
            act.activation(cond_act[:, :], cond_rows[:, :], ACT.Silu).then_inc(cond_ready, 1)
            act.activation(a_exp[:, :], alog_sb[:, :], ACT.Exp).then_inc(aexp_ready, 1)

            def load_table(func):
                return act.activation(probe[:, :], some, func)

            def first_tap(k):
                h = h_t[:, k.par, :]
                act.wait_ge(ht_ready, k.count(1, 1))
                if k.par == 1:
                    act.wait_ge(halo, (k.off // 2 + 1) if k.i is None else k.i + k.off // 2 + 1)
                act.activation(cv[:, 0, :], h[:, 0:CH], ACT.Identity, scale=convw_sb[:, 0:1]).then_inc(tap0_ready, 1)

            def modulate_prep(k):
                if k.par == 1:
                    act.activation(h_t[:, 1, 0:TAPS - 1], h_t[:, 0, CH:CH + TAPS - 1], ACT.Copy).then_inc(halo, 1)
                act.wait_ge(xnT1, k.count(1, 1))
                act.wait_ge(modp_set, (k.off // 2 + 1) if k.i is None else k.i + k.off // 2 + 1)
                act.activation(h_t[:, k.par, TAPS - 1:], misc[:, :], ACT.Identity, bias=mod_prep[:, 0:1],
                               scale=mod_prep[:, 1:2]).then_inc(ht_ready, 1)

            def conv_silu(k):
                act.wait_ge(conv_ready, k.count(1, 1))
                act.activation(xc[:, k.par, :], cv[:, 1, :], ACT.Silu, bias=vec[:, CONVB:CONVB + 1])\
                   .then_inc(xc_ready, 1)

            def softplus_ends(k):
                bias = vec[:, DTB:DTB + 1]
                act.wait_ge(zdt_ready, k.count(1, 1))
                act.activation(z_abs[:, :], misc[:, :], ACT.Abs, bias=bias).then_inc(zdt_abs, 1)
                act.activation(z_pos[:, :], misc[:, :], ACT.Relu, bias=bias).then_inc(zdt_used, 1)

            def softplus(k):
                act.wait_ge(zdt_abs, k.count(1, 1))
                act.activation(e_neg[:, :], z_abs[:, :], ACT.Exp, scale=-1.0).then_inc(eneg_ready, 1)
                act.wait_ge(eneg_ready, k.count(1, 1))
                act.activation(e_one, e_neg[:, :], ACT.Identity, bias=1.0).then_inc(eone_ready, 1)
                act.wait_ge(eone_ready, k.count(1, 1))
                act.activation(l_one[:, :], e_one, ACT.Ln).then_inc(lone_ready, 1)

            def split_high(k):
                act.wait_ge(bcp_ready, k.count(1, 1))
                act.activation(b_split[:, k.par, :], misc[0:96, :], ACT.Copy).then_inc(bhi_ready, 1)
                act.activation(c_rows[:, :], misc[0:32, :], ACT.Copy).then_inc(crow_ready, 1)

            def split_mid(k):
                act.wait_ge(brest_ready, k.count(1, 1))
                for lo, hi in ((32, 64), (64, 96)):
                    act.activation(b_split[lo:hi, k.par, :], b_rest[lo:hi, :], ACT.Copy).then_inc(bmid_ready, 1)

            def decays(k, first, end):
                if first == 0:
                    act.wait_ge(dt_ready, k.count(1, 1))
                    if k.i is None and k.off == 0:
                        act.wait_ge(mod_ps, 1)
                        act.wait_ge(sel_e, 2)
                for n in range(first, end):
                    if k.i is not None or k.off:
                        act.wait_ge(scan_done, k.count(NS, n + 1 - NS))
                    act.activation(decay[:, n, :], dt_sb[:, :], ACT.Exp, scale=a_neg[:, n:n + 1])\
                       .then_inc(decay_ready, 1)

            def u3_tile(k, j):
                m = width(j)
                act.wait_ge(p3_ready, k.count(JA, j + 1))
                if j >= 2:
                    act.wait_ge(z_done, k.count(JA, j - 1))
                act.activation(u3[0:m, j % 2, :], p3_bank[0:m, :], ACT.Identity, bias=vec[0:m, B3 + j:B3 + j + 1])\
                   .then_inc(u3_done, 1)

            def silu_tile(k, j):
                m = width(j)
                act.wait_ge(z_done, k.count(JA, j + 1))
                if j < JR:
                    dst = s_sb[0:m, j % 2, :]
                    if j >= 2:
                        act.wait_ge(hg_done, k.count(JR, j - 1))
                else:
                    dst = hg[0:m, j % HP, :]
                    act.wait_ge(w2_done, k.count(JA, j - HP + 1))
                act.activation(dst, z_sb[0:m, j % 2, :], ACT.Silu).then_inc(s_done, 1)

            act.wait_ge(aneg_ready, 1)
            some = vec[:, 0:1]
            act.wait_ge(vec_ready, 1)
            modulate_prep(Chunk(0))
            first_tap(Chunk(0))
            conv_silu(Chunk(0))
            softplus_ends(Chunk(0))
            split_high(Chunk(0))
            softplus(Chunk(0))
            split_mid(Chunk(0))

            def step(number, c):
                prep, scan, head, experts = stages(number)
                f, g, p = c.plus(-2), c.plus(-1), c.plus(1)
                if scan:
                    decays(c, DECAYS_0 if number else 0, DECAYS_1)
                if experts:
                    u3_tile(f, 1)
                if head:
                    act.wait_ge(x2_ready, g.count(1, 1))
                    act.wait_ge(st2_done, g.count(1, 1))
                    act.activation(x2[:, g.par, :], misc[:, :], ACT.Copy).then_inc(x2_done, 1)
                if scan:
                    decays(c, DECAYS_1, DECAYS_2)
                if head:
                    act.wait_ge(modm_set, (g.off // 2 + 1) if g.i is None else g.i + g.off // 2 + 1)
                    act.wait_ge(xnT2, g.count(1, 1))
                    act.activation(h2_t[:, :], misc[:, :], ACT.Identity, bias=mod_head[:, 0:1],
                                   scale=mod_head[:, 1:2]).then_inc(h2_ready, 1)
                if scan:
                    decays(c, DECAYS_2, NS)
                if prep:
                    normalise(0, x_sb[:, p.par, :, :], c.count(2, 4), xn1)
                load_table(ACT.Silu)
                for slot in range(1, JA + 1):
                    if experts:
                        if 2 <= slot < JA:
                            u3_tile(f, slot)
                        silu_tile(f, slot - 1)
                    if prep:
                        if slot == AT_HT:
                            modulate_prep(p)
                            first_tap(p)
                        if slot == AT_SILU:
                            conv_silu(p)
                        if slot == AT_ENDS:
                            softplus_ends(p)
                        if slot == AT_SPLIT:
                            split_high(p)
                    if slot == AT_SOFT and head:
                        act.wait_ge(ls_ready, g.count(1, 1))
                        act.activation(ge[:, :, :], ls[:, :, :], ACT.Exp).then_inc(ge_ready, 1)
                    if slot == AT_SOFT and prep:
                        softplus(p)
                    if slot == AT_MID and prep:
                        split_mid(p)
                if number == 0:
                    load_table(ACT.Exp).then_inc(out_ready, 1)
                if experts:
                    act.wait_ge(w2_done, f.count(JA, JA))
                    act.activation(v2, y_bank[:, :], ACT.Identity, bias=mod_tail[:, 1:2],
                                   scale=mod_tail[:, 0:1]).then_inc(v2_ready, 1)
                if head:
                    u3_tile(g, 0)
                if prep:
                    decays(p, 0, 2)
                if experts:
                    act.wait_ge(out_ps, f.count(1, 1))
                    if number >= NCH:
                        act.wait_ge(st_out, 16 * (number - 3))
                    act.activation(o_sb[:, f.par, :], misc[:, :], ACT.Copy).then_inc(out_ready, 1)
                if prep:
                    decays(p, 2, DECAYS_0)
                if head:
                    act.wait_ge(rwT_ready, g.count(1, 1))
                    act.activation(rw_t[:, g.par, :], y_bank[0:3 * E, :], ACT.Copy).then_inc(rwt_ready, 1)

            run(act, step)

        @block.tensor
        def _(pe):
            pe.wait_ge(id_set, 1)
            pe.wait_ge(wm_in, 16 * 13)
            pe.transpose(misc[:, 0:2 * NS + E], proj_rows[:, :], ident[0:2 * NS + E, 0:2 * NS + E])\
              .then_inc(projT, 1)
            pe.transpose(p3_bank[0:R, 0:P], dt_rows[:, :], ident[:, :]).then_inc(dtT, 1)
            pe.wait_ge(cond_ready, 1)
            pe.transpose(in_bank[0][:, 0:NB], cond_act[:, :], ident[0:NB, 0:NB]).then_inc(condT, 1)
            pe.wait_ge(wr_in, 16 * 10)
            pe.transpose(bc_bank[0][:, 0:32], vec_rows[:, :], ident[0:32, 0:32]).then_inc(vecT, 1)
            pe.wait_ge(dtt_ready, 1)
            pe.matmul(y_bank[:, 0:P], xdt_sb[:, :], dt_t[:, :], start=True, stop=True).then_inc(stepw_ps, 1)
            pe.wait_ge(condt_ready, 1)
            for j in range(6):
                mm = pe.matmul(p1_bank[:, NB * j:NB * j + NB], wmod_sb[:, j * P:(j + 1) * P], cond_t[:, :],
                               start=True, stop=True)
            mm.then_inc(mod_ps, 1)
            pe.wait_ge(vec_ready, 1)
            pe.wait_ge(proj_ready, 1)
            pe.wait_ge(mod_ready, 1)
            pe.wait_ge(bcw_ready, 1)
            pe.wait_ge(stepw_ready, 1)

            def tok_to_feat(src):
                for s in range(SUB):
                    mm = pe.transpose(misc[:, s * P:(s + 1) * P], src[:, s, :], ident[:, :])
                return mm

            def add_transposed(src, diag, last):
                for s in range(SUB):
                    mm = pe.matmul(misc[:, s * P:(s + 1) * P], src[:, s * P:(s + 1) * P], diag,
                                   start=False, stop=last and s == SUB - 1)
                return mm

            def step_sizes(k):
                pe.wait_ge(xc_ready, k.count(1, 1))
                pe.wait_ge(ht_ready, k.count(1, 1))
                pe.matmul(misc[:, :], step_w[:, :], xc[:, k.par, :], start=True, stop=True).then_inc(zdt_ready, 1)

            def bc_proj(k):
                pe.wait_ge(zdt_used, k.count(1, 1))
                pe.wait_ge(zdt_abs, k.count(1, 1))
                pe.matmul(misc[0:96, :], bc_w[:, :, :].rearrange("p a n -> p (a n)"), xc[:, k.par, :],
                          start=True, stop=True).then_inc(bcp_ready, 1)

            pe.wait_ge(xn1, 1)
            tok_to_feat(xn[:, 0, :, :]).then_inc(xnT1, 1)
            step_sizes(Chunk(0))
            bc_proj(Chunk(0))
            pe.wait_ge(sel_s, 3)

            def first_states(k, number):
                order = ring_order(number) if number >= 0 else []
                pe.wait_ge(b_ready, k.count(1, 1))
                for n in range(2):
                    if order:
                        assert order[n - 2][0] == "N"
                        pe.wait_ge(ub_done, k.plus(-1).count(NS, order[n - 2][1] + 1))
                    pe.matmul(bc_bank[(ring_start(number + 1) + n) % 2][:, :], sel_state[:, n, :],
                              b_split[:, k.par, :], start=True, stop=True).then_inc(bb_ready, 1)

            first_states(Chunk(0), -1)

            def step(number, c):
                prep, scan, head, experts = stages(number)
                f, g, p = c.plus(-2), c.plus(-1), c.plus(1)
                order = ring_order(number)
                before = ring_order(number - 1) if number else []
                start = ring_start(number)

                def ring(kind, n):
                    q = order.index((kind, n))
                    back = 1 if q < 2 else 0
                    if number or not back:
                        kind0, n0 = before[q - 2] if back else order[q - 2]
                        if kind0 == "N":
                            pe.wait_ge(ub_done, c.plus(-back).count(NS, n0 + 1))
                        else:
                            pe.wait_ge(hg_done, f.plus(-back).count(JR, n0 + 1))
                    return bc_bank[(start + q) % 2]

                def state(n):
                    if not scan:
                        return
                    to = ring("N", n)
                    pe.matmul(to[:, :], sel_state[:, n, :], b_split[:, c.par, :], start=True, stop=True)\
                      .then_inc(bb_ready, 1)

                def weight(j):
                    pe.matmul(ring("R", j)[:, :], sel_expert[:, j, :], rw_t[:, f.par, :], start=True, stop=True)\
                      .then_inc(rwb_ready, 1)

                def experts_in(f, j):
                    m = width(j)
                    if j:
                        pe.wait_ge(u3_done, f.count(JA, j))
                    for hi, lo, to, done in ((w3_hi, w3_lo, p3_bank, p3_ready), (w1_hi, w1_lo, p1_bank, p1_ready)):
                        if j and done is p1_ready:
                            pe.wait_ge(z_done, f.count(JA, j))
                        cols = slice(j * P, j * P + m)
                        pe.matmul(to[0:m, :], hi[:, cols], h2_hi[:, f.par, :], start=True, stop=False)
                        pe.matmul(to[0:m, :], hi[:, cols], h2_lo[:, f.par, :], start=False, stop=False)
                        pe.matmul(to[0:m, :], lo[:, cols], h2_hi[:, f.par, :], start=False, stop=True)\
                          .then_inc(done, 1)

                def experts_out(j):
                    m = width(j)
                    if j < JR:
                        pe.wait_ge(hg_done, f.count(JR, j + 1))
                    else:
                        pe.wait_ge(s_done, f.count(JA, j + 1))
                    pe.matmul(y_bank[:, :], w2_sb[0:m, j, :], hg[0:m, j % HP, :], start=(j == 0),
                              stop=(j == JA - 1)).then_inc(w2_done, 1)

                state(2)
                if head:
                    pe.wait_ge(diag_set, (g.off // 2 + 1) if g.i is None else g.i + g.off // 2 + 1)
                    pe.wait_ge(out_ready, f.count(1, 1) if number > 1 else 1)
                    pe.matmul(misc[:, :], ident[:, :], x_sb[:, g.par, :, :].rearrange("p s d -> p (s d)"),
                              start=True, stop=False).then_inc(x_used, 1)
                    add_transposed(xc[:, g.par, :], gate_diag[:, 1, :], False)
                state(3)
                if experts:
                    experts_in(f, 1)
                if head:
                    pe.wait_ge(acc_step, g.count(NS - 1, NS - 1))
                    add_transposed(acc[:, g.par, :], gate_diag[:, 0, :], True).then_inc(x2_ready, 1)
                state(4)
                state(5)
                state(6)
                state(7)
                if head:
                    pe.wait_ge(xn2, g.count(1, 1))
                    pe.wait_ge(x2_done, g.count(1, 1))
                    tok_to_feat(xn[:, 1, :, :]).then_inc(xnT2, 1)
                if head:
                    pe.wait_ge(h2_ready, g.count(1, 1))
                    for s in range(SUB):
                        mm = pe.matmul(misc[:, s * E:(s + 1) * E], h2_t[:, s * P:(s + 1) * P],
                                       proj_t[:, 2 * NS:2 * NS + E], start=True, stop=True)
                    mm.then_inc(lg_ready, 1)
                for slot in range(1, JA + 1):
                    if experts:
                        if 2 <= slot < JA:
                            experts_in(f, slot)
                        if slot <= JR:
                            if slot == 1:
                                pe.wait_ge(rwt_ready, f.count(1, 1))
                            weight(slot - 1)
                    if slot in SLOT_STATES:
                        state(SLOT_STATES[slot])
                    if experts:
                        if slot >= 2:
                            experts_out(slot - 2)
                        if slot == 3:
                            for q in range(3):
                                pe.matmul(y_bank[:, :], b2_part[:, q, :], rw_t[:, f.par, :], start=False, stop=False)
                    if prep:
                        if slot == AT_HT - 1:
                            pe.wait_ge(xn1, p.count(1, 1))
                            if head:
                                pe.wait_ge(ls_ready, g.count(1, 1))
                            else:
                                pe.wait_ge(brest_ready, p.count(1, 0))
                                pe.wait_ge(crow_ready, p.count(1, 0))
                            tok_to_feat(xn[:, 0, :, :]).then_inc(xnT1, 1)
                        if slot == AT_SILU:
                            step_sizes(p)
                        if slot == AT_ENDS:
                            bc_proj(p)
                if experts:
                    if prep:
                        pe.wait_ge(brest_ready, p.count(1, 1))
                        pe.wait_ge(crow_ready, p.count(1, 1))
                    elif not head:
                        pe.wait_ge(out_ready, f.count(1, 1))
                    pe.matmul(misc[:, :], ident[:, :], x2[:, f.par, :], start=True, stop=False)
                    experts_out(JA - 1)
                if head:
                    if number == 1:
                        pe.wait_ge(wsplit_ready, 2)
                        pe.wait_ge(w2_in, 16 * 3)
                        pe.wait_ge(sel_e, 2)
                        pe.wait_ge(b2_ready, 1)
                    pe.wait_ge(h2s_ready, g.count(1, 1))
                    if number > 1:
                        pe.wait_ge(u3_done, f.count(JA, JA))
                        pe.wait_ge(z_done, f.count(JA, JA))
                    experts_in(g, 0)
                if prep:
                    first_states(p, number)
                if experts:
                    pe.wait_ge(v2_ready, f.count(1, 1))
                    add_transposed(v2, ident[:, :], True).then_inc(out_ps, 1)
                if head:
                    pe.wait_ge(r3_ready, g.count(1, 1))
                    for s in range(SUB):
                        mm = pe.matmul(y_bank[0:3 * E, s * P:(s + 1) * P],
                                       rw_part[:, s, :, :].rearrange("p a e -> p (a e)"), ident_b[:, :],
                                       start=True, stop=True)
                    mm.then_inc(rwT_ready, 1)

            run(pe, step)

        @block.vector
        def _(dve):
            dve.memset(vec_rows[:, :], 0.0).then_inc(vz, 1)
            dve.memset(h_t[:, 0, 0:TAPS - 1], 0.0).then_inc(halo_set, 1)
            def moments_start(which, src):
                for s in range(SUB):
                    st = dve.bn_stats(stats[:, which, s, :], src[:, s, :])
                return st

            def moments_end(c, lo, hi):
                if lo == 0:
                    dve.wait_ge(st_done, c.count(1, 2))
                if hi == 2:
                    dve.wait_ge(st2_done, c.count(1, 0))
                alone(dve)
                for which in range(lo, hi):
                    for s in range(SUB):
                        ag = dve.bn_aggr(mv[:, which, s, :], stats[:, which, s, :])
                ag.then_inc(mv_done, 1)

            def variance(steps, lo, hi):
                dve.wait_ge(mv_done, steps)
                dve.tensor_scalar(ve[:, lo:hi, :], mv[:, lo:hi, :, 1], EPS, None, ALU.add).then_inc(ve_done, 1)

            def newton_1(steps, lo, hi):
                dve.wait_ge(r_done, steps)
                dve.tensor_tensor(nt[:, lo:hi, 0, :], r0[:, lo:hi, :], r0[:, lo:hi, :], ALU.mult).then_inc(nt_step, 1)

            def newton_2(steps, lo, hi):
                dve.wait_ge(nt_step, 2 * steps - 1)
                dve.scalar_tensor_tensor(nt[:, lo:hi, 1, :], nt[:, lo:hi, 0, :], -0.5, ve[:, lo:hi, :],
                                         ALU.mult, ALU.mult).then_inc(nt_step, 1)

            def newton_3(steps, lo, hi):
                dve.wait_ge(nt_step, 2 * steps)
                dve.scalar_tensor_tensor(rstd[:, lo:hi, :], nt[:, lo:hi, 1, :], 1.5, r0[:, lo:hi, :],
                                         ALU.add, ALU.mult).then_inc(rstd_done, 1)

            def shifts(steps, lo, hi):
                dve.wait_ge(rstd_done, 2 * steps - 1)
                dve.scalar_tensor_tensor(shift[:, lo:hi, :], mv[:, lo:hi, :, 0], -1.0, rstd[:, lo:hi, :],
                                         ALU.mult, ALU.mult).then_inc(rstd_done, 1)

            dve.wait_ge(x_in, 16)
            moments_start(0, x_sb[:, 0, :, :]).then_inc(st_done, 1)
            moments_end(Chunk(-1), 0, 1)
            for part in (variance, newton_1, newton_2, newton_3, shifts):
                part(1, 0, 1)

            dve.wait_ge(projT, 1)
            dve.tensor_copy(proj_t[:, :], misc[:, 0:2 * NS + E]).then_inc(proj_ready, 1)
            dve.wait_ge(dtT, 1)
            dve.tensor_copy(dt_t[:, :], p3_bank[0:R, 0:P]).then_inc(dtt_ready, 1)
            dve.wait_ge(condT, 1)
            dve.tensor_copy(cond_t[:, :], in_bank[0][:, 0:NB]).then_inc(condt_ready, 1)
            dve.wait_ge(vecT, 1)
            dve.tensor_copy(vec[:, :], bc_bank[0][:, 0:32]).then_inc(vec_ready, 1)
            dve.wait_ge(proj_ready, 1)
            for a in range(3):
                cp = dve.tensor_copy(bc_w[:, a, :], proj_t[:, 0:2 * NS])
            cp.then_inc(bcw_ready, 1)
            dve.wait_ge(stepw_ps, 1)
            dve.tensor_copy(step_w[:, :], y_bank[:, 0:P]).then_inc(stepw_ready, 1)
            dve.wait_ge(aexp_ready, 1)
            dve.tensor_scalar(a_neg[:, :], a_exp[:, :], -1.0, None, ALU.mult).then_inc(aneg_ready, 1)
            dve.wait_ge(mod_ps, 1)
            dve.tensor_copy(mod[:, :, :].rearrange("p j b -> p (j b)"), p1_bank[:, 0:6 * NB]).then_inc(mod_ready, 1)
            dve.wait_ge(mod_ready, 1)
            for a, j in enumerate((2, 5)):
                dve.tensor_scalar(sign[:, a, :], mod[:, j, :], 0.0, 2.0, ALU.is_ge, ALU.mult).then_inc(mod_a, 1)
                dve.wait_ge(mod_a, 3 * a + 1)
                dve.scalar_tensor_tensor(size[:, a, :], sign[:, a, :], -1.0, mod[:, j, :], ALU.add, ALU.mult)\
                   .then_inc(mod_a, 1)
                dve.wait_ge(mod_a, 3 * a + 2)
                dve.tensor_scalar(size[:, a, :], size[:, a, :], 0.25, None, ALU.max).then_inc(mod_a, 1)
            dve.wait_ge(mod_a, 6)
            dve.tensor_copy(mods[:, :, 0], mod[:, 0, :])
            dve.tensor_scalar(mods[:, :, 1], mod[:, 1, :], 1.0, None, ALU.add)
            dve.scalar_tensor_tensor(mods[:, :, 2], sign[:, 0, :], -1.0, size[:, 0, :], ALU.add, ALU.mult)
            dve.tensor_copy(mods[:, :, 4], mod[:, 3, :])
            dve.tensor_scalar(mods[:, :, 5], mod[:, 4, :], 1.0, None, ALU.add)
            dve.scalar_tensor_tensor(mods[:, :, 6], sign[:, 1, :], -1.0, size[:, 1, :], ALU.add, ALU.mult)\
               .then_inc(mod_b, 1)
            dve.wait_ge(mod_b, 1)
            dve.wait_ge(vec_ready, 1)
            dve.tensor_scalar(mods[:, :, 7], mods[:, :, 6], vec[:, SB2:SB2 + 1], None, ALU.mult)\
               .then_inc(mods_ready, 1)
            dve.tensor_scalar(mods[:, :, 3], mods[:, :, 2], vec[:, DPAR:DPAR + 1], None, ALU.mult).then_inc(mods_b, 1)
            dve.wait_ge(mods_ready, 1)
            dve.wait_ge(mods_b, 1)
            dve.tensor_copy(mod_prep[:, :], mods[:, 0, 0:2]).then_inc(modp_set, 1)
            dve.wait_ge(wm_in, 16 * 13)
            dve.tensor_copy(b2_part[:, 0, :], b2_rows[:, :]).then_inc(b2_a, 1)
            dve.wait_ge(b2_a, 1)
            dve.tensor_tensor(b2_rest[:, :], b2_rows[:, :], b2_part[:, 0, :], ALU.subtract).then_inc(b2_b, 1)
            dve.wait_ge(b2_b, 1)
            dve.tensor_copy(b2_part[:, 1, :], b2_rest[:, :]).then_inc(b2_c, 1)
            dve.wait_ge(b2_c, 1)
            dve.tensor_tensor(b2_part[:, 2, :], b2_rest[:, :], b2_part[:, 1, :], ALU.subtract).then_inc(b2_ready, 1)

            def convolve(k, t):
                h = h_t[:, k.par, :]
                if t == 1:
                    dve.wait_ge(tap0_ready, k.count(1, 1))
                else:
                    dve.wait_ge(conv_step, k.count(2, t - 1))
                dve.scalar_tensor_tensor(cv[:, t % 2, :], h[:, t:t + CH], convw_sb[:, t:t + 1],
                                         cv[:, (t - 1) % 2, :], ALU.mult, ALU.add)\
                   .then_inc(conv_step if t < TAPS - 1 else conv_ready, 1)

            def step_miss(k):
                dve.wait_ge(eone_ready, k.count(1, 1))
                dve.scalar_tensor_tensor(miss, e_one, 1.0, e_neg[:, :], ALU.subtract, ALU.subtract)\
                   .then_inc(miss_ready, 1)

            def step_size(k):
                dve.wait_ge(lone_ready, k.count(1, 1))
                dve.scalar_tensor_tensor(l_one[:, :], e_one, 1.0, l_one[:, :], ALU.is_gt, ALU.mult)\
                   .then_inc(lzero_ready, 1)
                dve.wait_ge(base_ready, k.count(1, 1))
                if k.i is not None or k.off:
                    dve.wait_ge(decay_ready, k.count(NS, 0))
                dve.wait_ge(lzero_ready, k.count(1, 1))
                dve.tensor_tensor(dt_sb[:, :], l_one[:, :], z_pos[:, :], ALU.add).then_inc(dt_ready, 1)

            def scan_input(k):
                dve.wait_ge(dt_ready, k.count(1, 1))
                dve.tensor_tensor(u_sb[:, k.par, :], dt_sb[:, :], xc[:, k.par, :], ALU.mult).then_inc(u_ready, 1)

            def b_remainder(k):
                dve.wait_ge(bhi_ready, k.count(1, 1))
                dve.wait_ge(crow_ready, k.count(1, 1))
                dve.tensor_tensor(b_rest[:, :], misc[0:96, :], b_split[:, k.par, :], ALU.subtract)\
                   .then_inc(brest_ready, 1)

            def b_low(k):
                dve.wait_ge(bmid_ready, k.count(2, 2))
                low = b_split[64:96, k.par, :]
                dve.tensor_tensor(low, b_rest[64:96, :], low, ALU.subtract).then_inc(b_ready, 1)

            for t in range(1, TAPS):
                convolve(Chunk(0), t)
            dve.wait_ge(w_in, 16 * 4)
            for part, whole in ((w1_m, w1_all), (w3_m, w3_all)):
                dve.tensor_scalar(part.bitcast(U32), whole.bitcast(U32), HIGH_BITS, None,
                                  ALU.bitwise_and).then_inc(whi_ready, 1)
            for q, (hi, lo, part, whole) in enumerate(((w1_hi, w1_lo, w1_m, w1_all),
                                                       (w3_hi, w3_lo, w3_m, w3_all))):
                dve.wait_ge(whi_ready, q + 1)
                dve.tensor_copy(hi[:, :], part)
                dve.tensor_tensor(lo[:, :], whole, part, ALU.subtract).then_inc(wsplit_ready, 1)
            dve.wait_ge(iota_set, 1)
            b_remainder(Chunk(0))
            step_miss(Chunk(0))
            b_low(Chunk(0))
            step_size(Chunk(0))
            scan_input(Chunk(0))

            def step(number, c):
                prep, scan, head, experts = stages(number)
                f, g, p = c.plus(-2), c.plus(-1), c.plus(1)
                order = ring_order(number)
                start = ring_start(number)

                def spread(kind, n):
                    return bc_bank[(start + order.index((kind, n))) % 2]

                def scan_state(n):
                    if not scan:
                        return
                    dve.wait_ge(ub_done, c.count(NS, n + 1))
                    dve.wait_ge(decay_ready, c.count(NS, n + 1))
                    if n >= HRING or number:
                        dve.wait_ge(cmul, c.count(NS, n - HRING + 1))
                    first = 0.0
                    if c.par == 1:
                        dve.wait_ge(carry_done, (c.off // 2 * NS + n + 1) if c.i is None
                                    else c.i * NS + (c.off // 2 * NS + n + 1))
                        first = carry[:, n:n + 1]
                    dve.tensor_tensor_scan(h_s[:, n % HRING, :], decay[:, n, :], in_bank[n % 2][:, :],
                                           first, ALU.mult, ALU.add).then_inc(scan_done, 1)

                def state_input(n):
                    if not scan:
                        return
                    if n == 0:
                        dve.wait_ge(u_ready, c.count(1, 1))
                    dve.wait_ge(bb_ready, c.count(NS, n + 1))
                    if n >= 2 or number:
                        dve.wait_ge(scan_done, c.count(NS, n - 1))
                    dve.tensor_tensor(in_bank[n % 2][:, :], u_sb[:, c.par, :], spread("N", n)[:, :], ALU.mult)\
                       .then_inc(ub_done, 1)

                def hidden(j):
                    if not experts:
                        return
                    m = width(j)
                    dve.wait_ge(u3_done, f.count(JA, j + 1))
                    dve.wait_ge(p1_ready, f.count(JA, j + 1))
                    if j >= 2:
                        dve.wait_ge(s_done, f.count(JA, j - 1))
                    dve.scalar_tensor_tensor(z_sb[0:m, j % 2, :], p1_bank[0:m, :],
                                             vec[0:m, B1 + j:B1 + j + 1], u3[0:m, j % 2, :],
                                             ALU.add, ALU.mult).then_inc(z_done, 1)

                def weigh(j):
                    if not experts:
                        return
                    dve.wait_ge(s_done, f.count(JA, j + 1))
                    dve.wait_ge(rwb_ready, f.count(JR, j + 1))
                    if j >= HP:
                        dve.wait_ge(w2_done, f.count(JA, j - HP + 1))
                    dve.tensor_tensor(hg[:, j % HP, :], s_sb[:, j % 2, :], spread("R", j)[:, :],
                                      ALU.mult).then_inc(hg_done, 1)

                def router(stage):
                    if not head or not 0 <= stage < ROUTER_STAGES:
                        return
                    if stage == 0:
                        dve.wait_ge(ge_ready, g.count(1, 1))
                        dve.tensor_reduce(gsum[:, :], ge[:, :, :], AX.X, ALU.add).then_inc(gsum_ready, 1)
                    elif stage == 1:
                        dve.wait_ge(gsum_ready, g.count(1, 1))
                        dve.reciprocal(grec[:, :], gsum[:, :]).then_inc(grec_ready, 1)
                    elif stage == 2:
                        dve.wait_ge(grec_ready, g.count(1, 1))
                        dve.tensor_tensor(score[:, :, :], ge[:, :, :],
                                          grec[:, :].unsqueeze(2).broadcast_to([P, SUB, E]), ALU.mult)\
                           .then_inc(score_ready, 1)
                    elif stage == 3:
                        dve.wait_ge(score_ready, g.count(1, 1))
                        dve.tensor_tensor(biased[:, :, :], score[:, :, :],
                                          gateb_sb[:, :].unsqueeze(1).broadcast_to([P, SUB, E]), ALU.add)\
                           .then_inc(biased_ready, 1)
                    elif stage == 4:
                        dve.wait_ge(biased_ready, g.count(1, 1))
                        alone(dve)
                        for s in range(SUB):
                            mx = dve.max(top[:, s, :], biased[:, s, :])
                        mx.then_inc(top_ready, 1)
                    elif stage == 5:
                        dve.wait_ge(top_ready, g.count(1, 1))
                        alone(dve)
                        for s in range(SUB):
                            mx = dve.max_index(topi[:, s, :], top[:, s, :], biased[:, s, :])
                        mx.then_inc(topi_ready, 1)
                    elif stage == 6:
                        dve.wait_ge(topi_ready, g.count(1, 1))
                        dve.tensor_copy(topf[:, :, :], topi[:, :, 0:2]).then_inc(topf_ready, 1)
                    elif stage == 7:
                        dve.wait_ge(topf_ready, g.count(1, 1))
                        for a in range(2):
                            eq = dve.tensor_tensor(hot[:, a, :, :],
                                                   iota_f[:, :].unsqueeze(1).broadcast_to([P, SUB, E]),
                                                   topf[:, :, a:a + 1].broadcast_to([P, SUB, E]), ALU.is_equal)
                        eq.then_inc(hot_ready, 1)
                    elif stage == 8:
                        dve.wait_ge(hot_ready, g.count(1, 1))
                        dve.tensor_tensor(hot[:, 0, :, :], hot[:, 0, :, :], hot[:, 1, :, :], ALU.add)\
                           .then_inc(hots_ready, 1)
                    elif stage == 9:
                        dve.wait_ge(hots_ready, g.count(1, 1))
                        dve.tensor_tensor(rw[:, :, :], score[:, :, :], hot[:, 0, :, :], ALU.mult)\
                           .then_inc(rw_ready, 1)
                    elif stage == 10:
                        dve.wait_ge(rw_ready, g.count(1, 1))
                        dve.tensor_copy(rw_part[:, :, 0, :], rw[:, :, :]).then_inc(rwh_ready, 1)
                    elif stage == 11:
                        dve.wait_ge(rwh_ready, g.count(1, 1))
                        dve.tensor_tensor(rw_rest[:, :, :], rw[:, :, :], rw_part[:, :, 0, :], ALU.subtract)\
                           .then_inc(rwr_ready, 1)
                    elif stage == 12:
                        dve.wait_ge(rwr_ready, g.count(1, 1))
                        dve.tensor_copy(rw_part[:, :, 1, :], rw_rest[:, :, :]).then_inc(rwm_ready, 1)
                    else:
                        dve.wait_ge(rwm_ready, g.count(1, 1))
                        dve.tensor_tensor(rw_part[:, :, 2, :], rw_rest[:, :, :], rw_part[:, :, 1, :],
                                          ALU.subtract).then_inc(r3_ready, 1)

                if number % 2 == 1:
                    if head:
                        b = g.off // 2 if g.i is None else g.i + g.off // 2
                        dve.tensor_copy(mod_gate[:, :], mods[:, b, 2:4]).then_inc(modg_set, 1)
                        dve.wait_ge(modg_set, (g.off // 2 + 1) if g.i is None else g.i + g.off // 2 + 1)
                        dve.tensor_scalar(gate_diag[:, 0, :], ident[:, :], mod_gate[:, 0:1], None, ALU.mult)
                        dve.tensor_scalar(gate_diag[:, 1, :], ident[:, :], mod_gate[:, 1:2], None, ALU.mult)\
                           .then_inc(diag_set, 1)
                    if prep:
                        b = p.off // 2 if p.i is None else p.i + p.off // 2
                        dve.tensor_copy(mod_prep[:, :], mods[:, b, 0:2]).then_inc(modp_set, 1)
                state_input(0)
                state_input(1)
                scan_state(0)
                hidden(0)
                state_input(2)
                scan_state(1)
                state_input(3)
                scan_state(2)
                lo, hi = 0 if prep else 1, 2 if head else 1
                normed = prep or head
                if head:
                    dve.wait_ge(x2_ready, g.count(1, 1))
                    moments_start(1, misc_t).then_inc(st2_done, 1)
                steps = c.count(1, 2)
                if head:
                    if number % 2 == 1:
                        b = g.off // 2 if g.i is None else g.i + g.off // 2
                        dve.tensor_copy(mod_head[:, :], mods[:, b, 4:6]).then_inc(modm_set, 1)
                    elif experts:
                        b = f.off // 2 if f.i is None else f.i + f.off // 2
                        dve.tensor_copy(mod_tail[:, :], mods[:, b, 6:8]).then_inc(modt_set, 1)
                state_input(4)
                scan_state(3)
                hidden(1)
                if prep:
                    dve.wait_ge(x_in, p.count(16, 16))
                    moments_start(0, x_sb[:, p.par, :, :]).then_inc(st_done, 1)
                if normed:
                    moments_end(c, lo, hi)
                    variance(steps, lo, hi)
                state_input(5)
                scan_state(4)
                if normed:
                    newton_1(steps, lo, hi)
                    newton_2(steps, lo, hi)
                    newton_3(steps, lo, hi)
                    shifts(steps, lo, hi)
                if head:
                    dve.wait_ge(x2_done, g.count(1, 1))
                    for s in range(SUB):
                        ts = dve.tensor_scalar(xn[:, 1, s, :], x2[:, g.par, s * P:(s + 1) * P], mv[:, 1, s, 0:1],
                                               rstd[:, 1, s:s + 1], ALU.subtract, ALU.mult)
                    ts.then_inc(xn2, 1)
                state_input(6)
                scan_state(5)
                state_input(7)
                scan_state(6)
                scan_state(7)
                if head:
                    dve.wait_ge(h2_ready, g.count(1, 1))
                    dve.tensor_scalar(h2_m.bitcast(U32), h2_t[:, :].bitcast(U32), HIGH_BITS, None,
                                      ALU.bitwise_and).then_inc(hh_ready, 1)
                    logits = misc[:, 0:SUB * E].rearrange("p (s e) -> p s e", s=SUB)
                    dve.wait_ge(lg_ready, g.count(1, 1))
                    dve.tensor_reduce(nmax[:, :], logits, AX.X, ALU.max, negate=True).then_inc(nmax_ready, 1)
                    dve.wait_ge(hh_ready, g.count(1, 1))
                    dve.tensor_copy(h2_hi[:, g.par, :], h2_m)
                    dve.tensor_tensor(h2_lo[:, g.par, :], h2_t[:, :], h2_m, ALU.subtract)\
                       .then_inc(h2s_ready, 1)
                    dve.wait_ge(nmax_ready, g.count(1, 1))
                    dve.tensor_tensor(ls[:, :, :], logits, nmax[:, :].unsqueeze(2).broadcast_to([P, SUB, E]),
                                      ALU.add).then_inc(ls_ready, 1)
                pending = None
                for slot in range(1, JA + 1):
                    stage = 3 * (slot - AT_SOFT) - 1
                    if 2 <= slot < JA:
                        hidden(slot)
                    router(stage)
                    if pending is not None:
                        scan_state(pending)
                        pending = None
                    router(stage + 1)
                    if slot <= JR:
                        weigh(slot - 1)
                    router(stage + 2)
                    if slot in SLOT_STATES:
                        pending = SLOT_STATES[slot]
                        state_input(pending)
                    if prep:
                        if slot == AT_MID + 1:
                            b_low(p)
                        if AT_CONV < slot < AT_CONV + TAPS:
                            convolve(p, slot - AT_CONV)
                        if slot == AT_SOFT:
                            b_remainder(p)
                            step_miss(p)
                        if slot == AT_SOFT + 1:
                            step_size(p)
                            scan_input(p)
                for stage in range(3 * (JA + 1 - AT_SOFT) - 1, ROUTER_STAGES):
                    router(stage)

            run(dve, step)


_INS = ['L0_attn_x', 'L0_attn_conv_w', 'L0_attn_conv_b', 'L0_attn_x_proj_dt_w', 'L0_attn_dt_proj_w',
        'L0_attn_dt_proj_b', 'L0_attn_B_proj_w', 'L0_attn_C_proj_w', 'L0_attn_A_log', 'L0_attn_D_param',
        'L0_ffn_gate_w', 'L0_ffn_gate_b', 'L0_ffn_w1', 'L0_ffn_b1', 'L0_ffn_w3', 'L0_ffn_b3', 'L0_ffn_w2',
        'L0_ffn_b2', 'L0_ffn_sw1', 'L0_ffn_sb1', 'L0_ffn_sw3', 'L0_ffn_sb3', 'L0_ffn_sw2', 'L0_ffn_sb2',
        'L0_c', 'L0_wmod']
_OUTS = [((4, 1024, 128), 'float32')]


def kernel(**inputs):
    import numpy as _np
    import concourse.bacc as _bacc
    from concourse import mybir as _mybir
    from concourse.bass_utils import run_bass_kernel_spmd as _run

    nc = _bacc.Bacc("TRN2", target_bir_lowering=False, num_devices=1)
    arrays, args = {}, []
    for name in _INS:
        a = _np.ascontiguousarray(inputs[name])
        arrays[f"in_{name}_dram"] = a
        args.append(nc.dram_tensor(f"in_{name}_dram", a.shape, _mybir.dt.from_np(a.dtype), kind="ExternalInput").ap())
    for i, (shape, dtype) in enumerate(_OUTS):
        dt = _mybir.dt.from_np(_np.dtype(dtype))
        args.append(nc.dram_tensor(f"out_{i}_dram", shape, dt, kind="ExternalOutput").ap())
    adaln_kernel(nc, *args)
    r = _run(nc, [arrays], core_ids=[0])
    got = tuple(r.results[0][f"out_{i}_dram"] for i in range(len(_OUTS)))
    return got[0]
```
